# Optimizing a Trainium2 kernel written in Bass

```python
import numpy as np
import jax
import jax.numpy as jnp

def _softmax(x, axis=-1):
    return jax.nn.softmax(x, axis=axis)

def _gelu(x):
    return jax.nn.gelu(x, approximate=True)

def _silu(x):
    return jax.nn.silu(x)

def _sigmoid(x):
    return jax.nn.sigmoid(x)

def _layernorm(x, axis=-1, eps=1e-05):
    m = jnp.mean(x, axis=axis, keepdims=True)
    v = jnp.var(x, axis=axis, keepdims=True)
    return (x - m) / jnp.sqrt(v + eps)

def _scatter_add(tgt, idx, src, axis=0):
    return tgt.at[idx].add(src)

def _segment_sum(src, seg, n):
    return jax.ops.segment_sum(src, seg, n)
kernel_name = 'mk_flamingo_gated_d1_seqx_r8_032073'

def setup_inputs(seed: int=0):
    np.random.seed(seed)
    _w = jnp.asarray

    def _rec_inputs():
        import jax
        import jax.numpy as jnp
        _rk = jax.random.key(seed)
        x = -0.0003929 + 0.9999 * jax.random.normal(jax.random.fold_in(_rk, 1), (32, 64, 512), jnp.float32)
        _lenS = 64 - jax.random.randint(jax.random.fold_in(_rk, 7), (32,), 0, max(1, 64 // 4) + 1, jnp.int32)
        _lenS2 = 64 - jax.random.randint(jax.random.fold_in(_rk, 8), (32,), 0, max(1, 64 // 4) + 1, jnp.int32)
        _ctx_4096P = jax.random.normal(jax.random.fold_in(_rk, 11), (32, 16, 512), jnp.float32)
        _ctx_4096c = jax.random.dirichlet(jax.random.fold_in(_rk, 511), 0.3 * jnp.ones((16,), jnp.float32), (32, 64))
        _ctx_4096t = jnp.einsum('bsk,bkd->bsd', _ctx_4096c, _ctx_4096P)
        _ctx_4096t = _ctx_4096t * jax.lax.rsqrt(jnp.mean(jnp.square(_ctx_4096t)) + 1e-12) * 0.953939
        ctx_4096 = 2.81802e-05 + 1.00001 * (_ctx_4096t + 0.3 * jax.random.normal(jax.random.fold_in(_rk, 611), (32, 64, 512), jnp.float32))
        _validS = jnp.arange(64)[None, :] < _lenS[:, None]
        _validS2 = jnp.arange(64)[None, :] < _lenS2[:, None]
        _causal = jnp.tril(jnp.ones((64, 64), dtype=bool))
        mask_BxSxS2_ff0 = jnp.where(jnp.ones((32, 64, 64), dtype=bool), 0.0, -1000000000.0).astype(jnp.float32)
        _g = jax.random.normal(jax.random.fold_in(_rk, 9001), (2, 1), jnp.float32)
        _g = jnp.sign(_g) * jnp.maximum(jnp.abs(_g), 1.0) + (_g == 0) * 1.0
        g_xattn = _g[0]
        g_ffn = _g[1]
        return (x, ctx_4096, mask_BxSxS2_ff0, g_xattn, g_ffn)
    x, ctx_4096, mask_BxSxS2_ff0, g_xattn, g_ffn = _rec_inputs()

    def _L0_xattn_setup():
        import jax, jax.numpy as jnp
        import numpy as np
        BS, SEQ, D_MODEL = (4, 128, 512)
        N_Q_HEADS, N_KV_HEADS, D_K, D_V = (32, 8, 128, 128)
        ROPE_BASE = 10000.0

        def _rotate_half(x):
            x1, x2 = jnp.split(x, 2, axis=-1)
            return jnp.concatenate([-x2, x1], axis=-1)

        def _apply_rope(x, pos0):
            d = x.shape[-1]
            seq = x.shape[2]
            inv_freq = 1.0 / ROPE_BASE ** (jnp.arange(0, d, 2, dtype=jnp.float32) / d)
            pos = (pos0 + jnp.arange(seq)).astype(jnp.float32)
            ang = pos[:, None] * inv_freq[None, :]
            cos = jnp.concatenate([jnp.cos(ang), jnp.cos(ang)], axis=-1)
            sin = jnp.concatenate([jnp.sin(ang), jnp.sin(ang)], axis=-1)
            return x * cos[None, None] + _rotate_half(x) * sin[None, None]
        key = jax.random.key(seed)
        ks = jax.random.split(key, 8)
        w_scale = 0.02
        return {'query': jax.random.normal(ks[0], (BS, SEQ, D_MODEL), dtype=jnp.float32), 'key': jax.random.normal(ks[1], (BS, SEQ, D_MODEL), dtype=jnp.float32), 'value': jax.random.normal(ks[2], (BS, SEQ, D_MODEL), dtype=jnp.float32), 'mask': jnp.zeros((BS, SEQ, SEQ), dtype=jnp.float32), 'wq': jax.random.normal(ks[3], (D_MODEL, N_Q_HEADS * D_K), dtype=jnp.float32) * w_scale, 'wk': jax.random.normal(ks[4], (D_MODEL, N_KV_HEADS * D_K), dtype=jnp.float32) * w_scale, 'wv': jax.random.normal(ks[5], (D_MODEL, N_KV_HEADS * D_V), dtype=jnp.float32) * w_scale, 'wo': jax.random.normal(ks[6], (N_Q_HEADS * D_V, D_MODEL), dtype=jnp.float32) * w_scale, 'curr_seq_pos': 0}
    _L0_xattn_all = _L0_xattn_setup()
    _L0_xattn_in = {k: v for k, v in _L0_xattn_all.items() if k in ('wq', 'wk', 'wv', 'wo')}
    del _L0_xattn_all

    def _L0_ffn_setup():
        import jax, jax.numpy as jnp
        import numpy as np
        R = 16
        LORA_ALPHA = 16
        SCALING = LORA_ALPHA / R
        key = jax.random.key(seed)
        kx, kr, ka = jax.random.split(key, 3)
        B, S, D, DO, E = (4, 256, 512, 512, 8)
        x = jax.random.normal(kx, (B, S, D), dtype=jnp.float32)
        bound_r = 1.0 / np.sqrt(D)
        route_w = jax.random.uniform(kr, (E, D), jnp.float32, -bound_r, bound_r)
        bound_a = 1.0 / np.sqrt(D)
        A = jax.random.uniform(ka, (E, R, D), jnp.float32, -bound_a, bound_a)
        kb = jax.random.fold_in(key, 7)
        Bw = jax.random.normal(kb, (E, DO, R), dtype=jnp.float32) * 0.02
        return {'x': x, 'route_w': route_w, 'A': A, 'Bw': Bw}
    _L0_ffn_all = _L0_ffn_setup()
    _L0_ffn_in = {k: v for k, v in _L0_ffn_all.items() if k in ('route_w', 'A', 'Bw')}
    del _L0_ffn_all
    return {'x': x, 'ctx_4096': ctx_4096, 'mask_BxSxS2_ff0': mask_BxSxS2_ff0, 'g_xattn': g_xattn, 'g_ffn': g_ffn, 'L0_xattn_wq': _L0_xattn_in['wq'], 'L0_xattn_wk': _L0_xattn_in['wk'], 'L0_xattn_wv': _L0_xattn_in['wv'], 'L0_xattn_wo': _L0_xattn_in['wo'], 'L0_ffn_route_w': _L0_ffn_in['route_w'], 'L0_ffn_A': _L0_ffn_in['A'], 'L0_ffn_Bw': _L0_ffn_in['Bw']}

def reference(x, ctx_4096, mask_BxSxS2_ff0, g_xattn, g_ffn, L0_xattn_wq, L0_xattn_wk, L0_xattn_wv, L0_xattn_wo, L0_ffn_route_w, L0_ffn_A, L0_ffn_Bw):
    import jax
    import jax.numpy as jnp

    def _L0_xattn_ref(query, key, value, mask, wq, wk, wv, wo, curr_seq_pos):
        import jax, jax.numpy as jnp
        import numpy as np
        BS, SEQ, D_MODEL = (4, 128, 512)
        N_Q_HEADS, N_KV_HEADS, D_K, D_V = (32, 8, 128, 128)
        ROPE_BASE = 10000.0

        def _rotate_half(x):
            x1, x2 = jnp.split(x, 2, axis=-1)
            return jnp.concatenate([-x2, x1], axis=-1)

        def _apply_rope(x, pos0):
            d = x.shape[-1]
            seq = x.shape[2]
            inv_freq = 1.0 / ROPE_BASE ** (jnp.arange(0, d, 2, dtype=jnp.float32) / d)
            pos = (pos0 + jnp.arange(seq)).astype(jnp.float32)
            ang = pos[:, None] * inv_freq[None, :]
            cos = jnp.concatenate([jnp.cos(ang), jnp.cos(ang)], axis=-1)
            sin = jnp.concatenate([jnp.sin(ang), jnp.sin(ang)], axis=-1)
            return x * cos[None, None] + _rotate_half(x) * sin[None, None]
        bs, sq, _ = query.shape
        n_groups = N_Q_HEADS // N_KV_HEADS
        q = (query @ wq).reshape(bs, sq, N_Q_HEADS, D_K).transpose((0, 2, 1, 3))
        sk = key.shape[1]
        k = (key @ wk).reshape(bs, sk, N_KV_HEADS, 1, D_K)
        k = jnp.repeat(k, n_groups, axis=3).reshape(bs, sk, N_Q_HEADS, D_K).transpose((0, 2, 1, 3))
        v = (value @ wv).reshape(bs, sk, N_KV_HEADS, 1, D_V)
        v = jnp.repeat(v, n_groups, axis=3).reshape(bs, sk, N_Q_HEADS, D_V).transpose((0, 2, 1, 3))
        scale = jnp.sqrt(jnp.float32(D_K))
        q = _apply_rope(q, curr_seq_pos)
        k = _apply_rope(k, curr_seq_pos)
        raw = jnp.einsum('bhqd,bhkd->bhqk', q, k) / scale
        masked = raw + mask[:bs, None, curr_seq_pos:curr_seq_pos + sq, :sk]
        attn = jax.nn.softmax(masked, axis=-1)
        out = jnp.einsum('bhqk,bhkd->bhqd', attn, v)
        out = out.transpose((0, 2, 1, 3)).reshape(bs, sq, N_Q_HEADS * D_V)
        return out @ wo

    def _L0_ffn_ref(x, route_w, A, Bw):
        import jax, jax.numpy as jnp
        import numpy as np
        R = 16
        LORA_ALPHA = 16
        SCALING = LORA_ALPHA / R
        logits = jnp.einsum('bsd,ed->bse', x, route_w)
        topk_v, topk_idx = jax.lax.top_k(logits, 1)
        E = logits.shape[-1]
        route_weight = jax.nn.one_hot(topk_idx[..., 0], E, dtype=logits.dtype) * topk_v
        h = jnp.einsum('bsd,erd->bser', x, A)
        wh = route_weight[..., None] * h
        out = jnp.einsum('bser,eor->bso', wh, Bw) * SCALING
        return out
    x = x + jnp.tanh(g_xattn[0]) * _L0_xattn_ref(_layernorm(x, axis=-1), ctx_4096, ctx_4096, mask_BxSxS2_ff0, L0_xattn_wq, L0_xattn_wk, L0_xattn_wv, L0_xattn_wo, 0)
    x = x + jnp.tanh(g_ffn[0]) * _L0_ffn_ref(_layernorm(x, axis=-1), L0_ffn_route_w, L0_ffn_A, L0_ffn_Bw)
    return x

_drawn_inputs = setup_inputs


def setup_inputs(seed=0):
    import zlib

    import numpy as np

    out = dict(_drawn_inputs(seed))
    spreads = {}
    factors = {'L0_xattn_wq': 3.615, 'L0_xattn_wk': 3.623}
    for name, (base, spread) in spreads.items():
        noise = np.random.default_rng([zlib.crc32(name.encode()), seed]).standard_normal(out[name].shape)
        drawn = base * np.exp(spread * noise) if base else spread * noise
        out[name] = jnp.asarray(drawn.astype(out[name].dtype))
    for name, factor in factors.items():
        out[name] = (out[name] * factor).astype(out[name].dtype)
    return out
```

```python
from contextlib import ExitStack

import numpy as np

import concourse.bass as bass
from concourse import mybir
from concourse.alu_op_type import AluOpType as ALU

F32 = mybir.dt.float32
F32R = mybir.dt.float32r
ACT = mybir.ActivationFunctionType
AX = mybir.AxisListType

P = 128
BATCH, SEQ, DM = 32, 64, 512
HEADS, KV_HEADS, DH = 32, 8, 128
EXPERTS, RANK = 8, 16
ROPE_BASE = 10000.0
LN_EPS = 1e-5

KT = DM // P
GROUP = HEADS // KV_HEADS
HALVES = 2
CHUNKS = 2
CHUNK = BATCH * SEQ // (HALVES * CHUNKS)
CHUNK_TILES = CHUNK // P
HALF_TILES = CHUNKS * CHUNK_TILES
CHUNK_SEQS = CHUNK // SEQ
SUBS = 2
SUB_SEQS = CHUNK_SEQS // SUBS
PAIRS = SUB_SEQS // 2
HEAD_PAIRS = GROUP // 2
ER = EXPERTS * RANK
ROUTED = EXPERTS + ER

COS, SIN, IDENT, RANKS = 0, SEQ, 2 * SEQ, 2 * SEQ + P
TABLE = RANKS + EXPERTS


class Mark:

    def __init__(self, sem, time):
        self.sem, self.value, self.time = sem, None, time


class Plan:

    def __init__(self, nc, ctx):
        self.nc, self.ctx = nc, ctx
        self.queues = {"sync": [], "tensor": [], "vector": [], "scalar": [], "gpsimd": []}
        self.sems, self.counts, self.owner = {}, {}, {}
        self.order = 0

    def put(self, engine, time, emit, waits=(), signal=None, step=1, cost=None):
        waits = [w for w in waits if w is not None]
        time = max([time] + [w.time for w in waits])
        cost = COST[engine] if cost is None else cost
        mark = None
        if signal is not None:
            if signal not in self.sems:
                self.sems[signal] = self.ctx.enter_context(self.nc.semaphore(signal))
                self.owner[signal] = engine
            assert self.owner[signal] == engine, signal
            mark = Mark(signal, time + cost)
        self.queues[engine].append((time, self.order, emit, waits, mark, step))
        self.order += 1
        return mark

    def count(self):
        for queue in self.queues.values():
            queue.sort(key=lambda q: (q[0], q[1]))
            for _, _, _, _, mark, step in queue:
                if mark is not None:
                    self.counts[mark.sem] = self.counts.get(mark.sem, 0) + step
                    mark.value = self.counts[mark.sem]

    def emit(self, engine, eng):
        passed = {}
        for _, _, emit, waits, mark, step in self.queues[engine]:
            need = {}
            for w in waits:
                need[w.sem] = max(need.get(w.sem, 0), w.value)
            for sem, value in need.items():
                if passed.get(sem, 0) < value:
                    eng.wait_ge(self.sems[sem], value)
                    passed[sem] = value
            last = emit(eng)
            if mark is not None:
                last.then_inc(self.sems[mark.sem], step)


T_MM = 0.2135
COST = {"sync": 2.5, "vector": .7, "scalar": .6, "gpsimd": 1.3}
T_SMALL = 0.2
T_COPY = 0.65
T_POOL = 1.3
T_DMA = 3.0
T_SEM = 0.15


def build(nc, x, ctx_in, mask, g_attn, g_ffn, wq, wk, wv, wo, route_w, lora_a, lora_b, table, out):
    RAW = 6
    STAGE = 4
    WO_SLOTS = GROUP + 1
    Q_SLOTS = 6

    x_tiles = x.rearrange("b s d -> (b s) d").rearrange("(t p) d -> t p d", p=P)
    ctx_tiles = ctx_in.rearrange("b s d -> (b s) d").rearrange("(t p) d -> t p d", p=P)
    out_tiles = out.rearrange("b s d -> (b s) d").rearrange("(t p) d -> t p d", p=P)
    wq_rows = wq.rearrange("(k p) n -> p k n", p=P)
    wk_rows = wk.rearrange("(k p) n -> p k n", p=P)
    wv_rows = wv.rearrange("(k p) n -> p k n", p=P)

    stack = ExitStack()
    with stack:
        def sb(name, shape, dt=F32):
            return stack.enter_context(nc.sbuf_tensor(name, shape, dt))

        def ps(name):
            return stack.enter_context(nc.psum_tensor(name, [P, 512], F32))

        xT = [sb(f"xT{c}", [P, 2, KT, CHUNK], F32R) for c in range(CHUNKS)]
        ctxT = [sb(f"ctxT{c}", [P, 2, KT, CHUNK], F32R) for c in range(CHUNKS)]
        wq_s = [sb(f"wq_s{j}", [P, 2, KT, DH], F32R) for j in range(GROUP)]
        wk_s = sb("wk_s", [P, 2, KT, DH], F32R)
        wv_s = sb("wv_s", [P, 2, KT, 2 * DH], F32R)
        wo_s = [sb(f"wo_s{j}", [P, 2, DM], F32R) for j in range(WO_SLOTS)]
        o_s = sb("o_s", [P, 2, PAIRS, GROUP, P], F32R)
        raw = sb("raw", [P, RAW, 512])
        stage = sb("stage", [P, STAGE, DM])
        acc = sb("acc", [P, HALF_TILES, DM])
        rot = sb("rot", [P, 2, CHUNK])
        q_r = sb("q_r", [P, Q_SLOTS // 2, CHUNK_SEQS, 2, SEQ])
        k_r = sb("k_r", [P, 2, CHUNK])
        v_sb = sb("v_sb", [P, HALF_TILES, 2 * DH])
        prob = sb("prob", [P, 2, 512])
        probT = sb("probT", [P, 2, 512])
        mask_sb = sb("mask_sb", [P, BATCH, SEQ])
        tab = sb("tab", [P, TABLE])
        routedT = sb("routedT", [P, KT, ROUTED])
        lora_bT = sb("lora_bT", [P, DM])
        gates = sb("gates", [P, 2])
        gates_t = sb("gates_t", [P, 2])
        stats = sb("stats", [P, 4, 6])
        moments = sb("moments", [P, 4, 2])
        var_eps = sb("var_eps", [P, 4])
        rstd = sb("rstd", [P, 4])
        power = sb("power", [P, 1])
        neg_max = sb("neg_max", [P, 2, HEAD_PAIRS * SUB_SEQS])
        row_sum = sb("row_sum", [P, 2, HEAD_PAIRS * SUB_SEQS])
        row_inv = sb("row_inv", [P, 2, HEAD_PAIRS * SUB_SEQS])
        top = sb("top", [P, 2, 2 + 2 * EXPERTS])
        whT = sb("whT", [P, P])

        proj = [ps("proj0"), ps("proj1")]
        score = ps("score")
        turned = ps("turned")
        attn = [ps("attn0"), ps("attn1")]
        y = [ps("y0"), ps("y1")]

        plan = Plan(nc, stack)
        put = plan.put
        ident = tab[:, IDENT:IDENT + P]

        def dma(dst, src):
            return lambda e: e.dma_start(dst, src)

        table_in = put("sync", -99, dma(tab[:, :], table), signal="table_in", step=16)
        put("scalar", -99, dma(gates[:, 0:1], g_attn.rearrange("(a n) -> a n", a=1).to_broadcast([P, 1])),
            signal="gates_in", step=16)
        gates_in = put("scalar", -99, dma(gates[:, 1:2], g_ffn.rearrange("(a n) -> a n", a=1).to_broadcast([P, 1])),
                       signal="gates_in", step=16)
        mask_in = None
        for b0 in range(0, BATCH, CHUNK_SEQS):
            for twin in range(2):
                mask_in = put("scalar", -98, dma(mask_sb[64 * twin:64 * twin + 64, b0:b0 + CHUNK_SEQS, :],
                                                 mask[b0:b0 + CHUNK_SEQS].rearrange("b q k -> q b k")),
                              signal="mask_in", step=16)
        gates_ready = put("scalar", 2, lambda e: e.activation(gates_t[:, :], gates[:, :], ACT.Tanh),
                          [gates_in], "gates_ready")
        power_set = put("gpsimd", -99, lambda e: e.memset(power[:, :], -0.5), signal="power_set")

        ln_count = [0]
        ln_done = []

        def layer_norm(t, src, dst, waits):
            i = ln_count[0] % 4
            ln_count[0] += 1
            s = put("vector", t, lambda e: e.bn_stats(stats[:, i, :], src), waits, "ln_stats")
            m = put("vector", t + T_COPY, lambda e: e.bn_aggr(moments[:, i, :], stats[:, i, :]), [s], "ln_moments", cost=T_SMALL)
            v = put("vector", t + T_COPY + .2, lambda e: e.tensor_scalar(
                var_eps[:, i:i + 1], moments[:, i, 1:2], LN_EPS, None, ALU.add), [m], "ln_var", cost=T_SMALL)
            r = put("gpsimd", t + T_COPY + .5, lambda e: e.tensor_tensor(
                rstd[:, i:i + 1], var_eps[:, i:i + 1], power[:, :], ALU.pow),
                [v, power_set] + ln_done[-4:-3], "ln_rstd", cost=.5)
            n = put("vector", t + T_COPY + 1.4, lambda e: e.tensor_scalar(
                dst, src, moments[:, i, 0:1], rstd[:, i:i + 1], ALU.subtract, ALU.mult), [r], "ln_done")
            ln_done.append(n)
            return n

        now = [0.0]
        drained = []
        drain_time = [0.0]

        def on_tensor(duration, emit, waits, signal):
            mark = put("tensor", now[0], emit, waits, signal, cost=duration)
            now[0] = mark.time
            return mark

        def fill(duration, emit, waits):
            n = len(drained)
            bank = proj[n % 2]
            drained.append(None)
            mark = on_tensor(duration, lambda e: emit(e, bank), list(waits) + [drained[n - 2] if n >= 2 else None],
                             "proj_filled")
            return n, bank, mark

        def drain(n, t, emit, waits):
            drain_time[0] = max(drain_time[0] + .001, t)
            drained[n] = put("vector", drain_time[0], emit, waits, "proj_drained")
            return drained[n]

        def turn(src, rows, cols, waits):
            def emit(e, bank):
                for k in range(cols):
                    last = e.transpose(bank[:, k * rows:(k + 1) * rows], src[:, k * P:(k + 1) * P],
                                       ident[0:rows, 0:rows])
                return last
            return fill(.25, emit, list(waits) + [table_in])

        stage_free = [None] * STAGE
        stage_count = [0]
        part_ready = {}
        chunk_free = {}

        def take_stage():
            slot = stage_count[0] % STAGE
            stage_count[0] += 1
            free = stage_free[slot]
            assert free != "taken"
            stage_free[slot] = "taken"
            return slot, free

        def load_tile(kind, index, tt, t):
            slot, free = take_stage()
            src = (x_tiles if kind == "x" else ctx_tiles)[index * CHUNK_TILES + tt]
            here = stage[:, slot, :]
            loaded = put("sync", t, dma(here, src), [free], f"stage_in{slot}", 16)
            if kind == "x":
                loaded = layer_norm(t + T_DMA, here, here, [loaded])
            return slot, loaded

        def turn_tile(kind, index, tt, slot, loaded):
            dst = (xT if kind == "x" else ctxT)[index % CHUNKS]
            n, bank, filled = turn(stage[:, slot, :], P, KT, [loaded])
            stage_free[slot] = filled
            src = bank[:, :].rearrange("p (k t) -> p k t", k=KT)
            high, low = (dst[:, part, :, tt * P:(tt + 1) * P] for part in (0, 1))
            t = now[0] + T_SEM
            h = put("scalar", t, lambda e: e.activation(high, src, ACT.Copy),
                    [filled, chunk_free.get((kind, index % CHUNKS))], "tile_high")
            low_done = drain(n, t + T_COPY + T_SEM, lambda e: e.tensor_tensor(low, src, high.bitcast(F32), ALU.subtract),
                             [h])
            part_ready.setdefault((kind, index), []).append(low_done)

        raw_free = [None] * RAW
        raw_count = [0]

        def fetch(t, src, shape, high, low, free, low_engine="gpsimd"):
            slot = raw_count[0] % RAW
            raw_count[0] += 1
            here = raw[:, slot, :] if shape is None else raw[:, slot, :].rearrange("p (k n) -> p k n", k=shape)
            loaded = put("sync", t - 6, dma(here, src), [raw_free[slot]], f"raw_in{slot}", 16)
            h = put("scalar", t, lambda e: e.activation(high, here, ACT.Copy), [loaded, free], "weight_high")
            raw_free[slot] = put(low_engine, t + T_COPY + T_SEM,
                                 lambda e: e.tensor_tensor(low, here, high.bitcast(F32), ALU.subtract), [h],
                                 f"weight_low_{low_engine}")
            return raw_free[slot]

        GROUPS = HALVES * KV_HEADS
        wq_ready, wk_ready, wv_ready, wo_ready = {}, {}, {}, {}

        def fetch_wq(t, G, j, free=None):
            col = ((G % KV_HEADS) * GROUP + j) * DH
            wq_ready[G, j] = fetch(t, wq_rows[:, :, col:col + DH], KT, wq_s[j][:, 0], wq_s[j][:, 1], free)

        def fetch_wk(t, G, free=None):
            col = (G % KV_HEADS) * DH
            wk_ready[G] = fetch(t, wk_rows[:, :, col:col + DH], KT, wk_s[:, 0], wk_s[:, 1], free)

        def fetch_wv(t, G, free=None):
            col = (G % KV_HEADS) * DH
            for k in (0, 2):
                wv_ready[G] = fetch(t, wv_rows[:, k:k + 2, col:col + 2 * DH], 2, wv_s[:, 0, k:k + 2],
                                    wv_s[:, 1, k:k + 2], free)
                t += T_POOL + .1

        def fetch_wo(t, n, free=None):
            row = (n % HEADS) * DH
            w = wo_s[n % WO_SLOTS]
            wo_ready[n] = fetch(t, wo[row:row + DH, :], None, w[:, 0], w[:, 1], free, "vector")

        def unit(u):
            G, c = divmod(u, CHUNKS)
            return G, c, (G // KV_HEADS) * CHUNKS + c

        def three_products(e, bank, stationary, moving):
            pairs = [(0, 0), (0, 1), (1, 0)]
            for k in range(KT):
                for i, (a, b) in enumerate(pairs):
                    last = e.matmul(bank, stationary(a, k), moving(b, k), start=(k == 0 and i == 0),
                                    stop=(k == KT - 1 and i == 2))
            return last

        rope_added = []
        roped = {}
        scored = {}
        values_used = {}

        def rope(n, bank, filled, dst, dst_free):
            i = len(rope_added)
            r = rot[:, i % 2, :]
            free = rope_added[i - 2] if i >= 2 else None
            t = now[0] + T_SEM
            half = DH // 2
            a = put("scalar", t, lambda e: e.activation(r[0:half, :], bank[half:DH, :], ACT.Copy), [filled, free],
                    "rotated")
            a = put("scalar", t + .5, lambda e: e.activation(r[half:DH, :], bank[0:half, :], ACT.Copy), [a], "rotated")
            per_seq = [P, CHUNK_SEQS, SEQ]
            cos = tab[:, COS:COS + SEQ].unsqueeze(1).to_broadcast(per_seq)
            sin = tab[:, SIN:SIN + SEQ].unsqueeze(1).to_broadcast(per_seq)
            src, r3 = (v.rearrange("p (b s) -> p b s", s=SEQ) for v in (bank[:, :], r))
            s = put("gpsimd", t + 1.4, lambda e: e.tensor_tensor(r3, r3, sin, ALU.mult), [a, table_in], "rotated_sin")
            c = drain(n, t + 1.4, lambda e: e.tensor_tensor(dst, src, cos, ALU.mult), [a, dst_free, table_in])
            done = put("vector", t + 1.4 + T_POOL + .3, lambda e: e.tensor_tensor(dst, dst, r3, ALU.add), [s, c],
                       "rope_added")
            rope_added.append(done)
            return done

        def project_k(u):
            G, c, index = unit(u)
            n, bank, filled = fill(12 * T_MM, lambda e, bank: three_products(
                e, bank[:, :], lambda a, k: wk_s[:, a, k, :], lambda b, k: ctxT[c][:, b, k, :]),
                [wk_ready[G]] + part_ready["ctx", index])
            roped[u, "k"] = rope(n, bank, filled, k_r[:, u % 2, :].rearrange("p (b s) -> p b s", s=SEQ), scored.get(SUBS * (u - 2) + 1))
            chunk_free["ctx", c] = filled
            if c == CHUNKS - 1 and G + 1 < GROUPS:
                fetch_wk(now[0] + 2, G + 1, filled)

        def q_slot(u, j):
            return (GROUP * u + j) % Q_SLOTS

        def project_q(u, j):
            G, c, index = unit(u)
            before = GROUP * u + j - Q_SLOTS
            free = scored.get(SUBS * (before // GROUP) + 1)
            n, bank, filled = fill(12 * T_MM, lambda e, bank: three_products(
                e, bank[:, :], lambda a, k: wq_s[j][:, a, k, :], lambda b, k: xT[c][:, b, k, :]),
                [wq_ready[G, j]] + part_ready["x", index])
            roped[u, j] = rope(n, bank, filled, q_r[:, q_slot(u, j) // 2, :, j % 2, :], free)
            chunk_free["x", c] = filled
            if c == CHUNKS - 1 and G + 1 < GROUPS:
                fetch_wq(now[0] + 3, G + 1, j, filled)

        v_ready = {}

        def project_v(u, tt):
            G, c, index = unit(u)
            n, bank, filled = fill(12 * T_MM / 2, lambda e, bank: three_products(
                e, bank[:, 0:2 * DH], lambda a, k: ctxT[c][:, a, k, tt * P:(tt + 1) * P],
                lambda b, k: wv_s[:, b, k, :]), [wv_ready[G]] + part_ready["ctx", index])
            chunk_free["ctx", c] = filled
            tile = c * CHUNK_TILES + tt
            v_ready[G // 2, tile] = drain(n, now[0] + T_SEM, lambda e: e.tensor_copy(v_sb[:, tile, :], bank[:, 0:2 * DH]),
                                          [filled, values_used.get(SUBS * (u - 2) + 1)])
            if c == CHUNKS - 1 and tt == CHUNK_TILES - 1 and G + 2 < GROUPS:
                fetch_wv(now[0] + 8, G + 2, filled)

        masked, turned_copied, low_made, normalised = {}, {}, {}, {}
        wo_used = {}
        y_count = [0]
        y_added = []
        acc_loaded, x1_ready = {}, {}

        def scores(k):
            u, s = divmod(k, SUBS)
            G, c, index = unit(u)

            def emit(e):
                for hp in range(HEAD_PAIRS):
                    for b in range(SUB_SEQS):
                        tok = (s * SUB_SEQS + b) * SEQ
                        col = (hp * SUB_SEQS + b) * SEQ
                        last = e.matmul(score[:, col:col + SEQ], q_r[:, q_slot(u, 2 * hp) // 2, s * SUB_SEQS + b, :, :].rearrange("p h s -> p (h s)"),
                                        k_r[:, u % 2, tok:tok + SEQ], start=True, stop=True)
                return last
            scored[k] = on_tensor(8 * 4 * T_MM / 8, emit,
                                  [roped[u, w] for w in ("k", *range(GROUP))] + [masked.get(k - 1)], "scored")
            t = now[0] + T_SEM
            i = k % 2
            rows = HEAD_PAIRS * SUB_SEQS
            p = prob[:, i, :]
            p3 = p.rearrange("p (r k) -> p r k", r=rows)
            seq0 = index * CHUNK_SEQS + s * SUB_SEQS
            m_ap = mask_sb[:, seq0:seq0 + SUB_SEQS, :].rearrange("p b k -> p (b k)").unsqueeze(1).to_broadcast(
                [P, HEAD_PAIRS, SUB_SEQS * SEQ])
            masked[k] = put("vector", t, lambda e: e.scalar_tensor_tensor(
                out=p.rearrange("p (h n) -> p h n", h=HEAD_PAIRS), in0=score[:, :].rearrange("p (h n) -> p h n", h=HEAD_PAIRS),
                scalar=float(1.0 / np.sqrt(np.float32(DH))), in1=m_ap, op0=ALU.mult, op1=ALU.add),
                [scored[k], mask_in, probs_turned.get(k - 2)], "masked")
            t += T_COPY
            a = put("vector", t, lambda e: e.tensor_reduce(neg_max[:, i, :], p3, AX.X, ALU.max, negate=True),
                    [masked[k]], "neg_max")
            t += T_COPY + T_SEM
            b = put("gpsimd", t, lambda e: e.tensor_tensor(
                p3, p3, neg_max[:, i, :].unsqueeze(2).to_broadcast([P, rows, SEQ]), ALU.add), [a], "shifted")
            t += T_POOL + T_SEM
            ex = put("scalar", t, lambda e: e.activation(p, p, ACT.Exp), [b], "exponentials")
            t += T_COPY + T_SEM
            sm = put("vector", t, lambda e: e.tensor_reduce(row_sum[:, i, :], p3, AX.X, ALU.add), [ex], "row_sum")
            inv = put("vector", t + T_COPY, lambda e: e.reciprocal(row_inv[:, i, :], row_sum[:, i, :]), [sm], "row_inv", cost=T_SMALL)
            t += T_COPY + .3
            normalised[k] = put("gpsimd", t, lambda e: e.tensor_tensor(
                p3, p3, row_inv[:, i, :].unsqueeze(2).to_broadcast([P, rows, SEQ]), ALU.mult), [inv], "normalised")

        probs_turned = {}

        def turn_probs(k):
            i = k % 2

            def emit(e):
                for bp in range(PAIRS):
                    for hp in range(HEAD_PAIRS):
                        src = (hp * PAIRS + bp) * P
                        dst = (bp * HEAD_PAIRS + hp) * P
                        last = e.transpose(turned[:, dst:dst + P], prob[:, i, src:src + P], ident)
                return last
            probs_turned[k] = on_tensor(.25, emit, [normalised[k], turned_copied.get(k - 1)], "probs_turned")
            turned_copied[k] = put("scalar", now[0] + T_SEM, lambda e: e.activation(probT[:, i, :], turned[:, :], ACT.Copy),
                                   [probs_turned[k], values_used.get(k - 2)], "turned_copied")

        def times_values(k):
            u, s = divmod(k, SUBS)
            G, c, index = unit(u)
            i = k % 2
            for twin in range(2):
                rows = slice(64 * twin, 64 * twin + 64)

                def emit(e, rows=rows, twin=twin):
                    for bp in range(PAIRS):
                        tile = c * CHUNK_TILES + s * PAIRS + bp
                        last = e.matmul(attn[twin][:, bp * 256:(bp + 1) * 256],
                                        v_sb[rows, tile, (G % 2) * DH:(G % 2 + 1) * DH],
                                        probT[rows, i, bp * 256:(bp + 1) * 256], start=True, stop=True)
                    return last
                tile = c * CHUNK_TILES + s * PAIRS
                values_used[k] = on_tensor(2 * 4 * T_MM / 2, emit,
                                           [turned_copied[k], low_made.get((k - 1, twin))] +
                                           [v_ready[G // 2, tile + bp] for bp in range(PAIRS)], "values_used")
                t = now[0] + T_SEM
                src = attn[twin][:, :].rearrange("p (b h q) -> p b h q", b=PAIRS, h=GROUP)
                high, low = (o_s[:, part, :, :, 64 * twin:64 * twin + 64] for part in (0, 1))
                h = put("scalar", t, lambda e, high=high, src=src: e.activation(high, src, ACT.Copy),
                        [values_used[k], y_used.get(k - 1)], "out_high")
                low_made[k, twin] = put("vector", t + T_COPY + T_SEM, lambda e, high=high, low=low, src=src:
                                        e.tensor_tensor(low, src, high.bitcast(F32), ALU.subtract), [h], "out_low")

        y_used = {}

        def project_out(k, bp):
            u, s = divmod(k, SUBS)
            G, c, index = unit(u)
            bank = y[y_count[0] % 2]
            free = y_added[y_count[0] - 2] if y_count[0] >= 2 else None
            y_count[0] += 1
            last_use = c == CHUNKS - 1 and s == SUBS - 1 and bp == PAIRS - 1
            for h in range(GROUP):
                n = G * GROUP + h
                w = wo_s[n % WO_SLOTS]

                def emit(e, h=h, w=w):
                    for i, (a, b) in enumerate(((0, 0), (0, 1), (1, 0))):
                        last = e.matmul(bank[:, :], o_s[:, a, bp, h, :], w[:, b, :], start=(h == 0 and i == 0),
                                        stop=(h == GROUP - 1 and i == 2))
                    return last
                used = on_tensor(3 * T_MM, emit, [wo_ready[n], low_made[k, 0], low_made[k, 1], free], "out_projected")
                if last_use and n + WO_SLOTS < GROUPS * GROUP:
                    fetch_wo(now[0] + .2, n + WO_SLOTS, used)
            y_used[k] = used
            tile = c * CHUNK_TILES + s * PAIRS + bp
            half = G // KV_HEADS
            here = acc[:, tile, :]
            done = put("vector", now[0] + T_SEM, lambda e: e.scalar_tensor_tensor(
                out=here, in0=bank[:, :], scalar=gates_t[:, 0:1], in1=here, op0=ALU.mult, op1=ALU.add),
                [used, gates_ready, acc_loaded[half, tile], x1_ready.get((half, tile))], "y_added")
            y_added.append(done)
            x1_ready[half, tile] = done

        expert = {}
        whT_free = [None]
        x2T_free = [None]
        stores = []

        def expert_norm(half, tile, t):
            slot, free = take_stage()
            loaded = layer_norm(t, acc[:, tile, :], stage[:, slot, :], [x1_ready[half, tile], free])
            expert[half, tile] = [slot, loaded]

        def expert_turn(half, tile):
            slot, loaded = expert[half, tile]
            n, bank, filled = turn(stage[:, slot, :], P, KT, [loaded])
            copied = drain(n, now[0] + T_SEM, lambda e: e.tensor_copy(stage[:, slot, :], bank[:, :]), [filled])
            expert[half, tile] = [slot, copied]

        def expert_route(half, tile):
            slot, copied = expert[half, tile]

            def emit(e, bank):
                for k in range(KT):
                    last = e.matmul(bank[:, 0:ROUTED], stage[:, slot, k * P:(k + 1) * P], routedT[:, k, :],
                                    start=(k == 0), stop=(k == KT - 1))
                return last
            n, bank, filled = fill(KT * 4 * ROUTED / 2400, emit, [copied, experts_ready])
            i = tile % 2
            best, rank = top[:, i, 0:1], top[:, i, 1:2]
            ranks, weight = top[:, i, 2:2 + EXPERTS], top[:, i, 2 + EXPERTS:2 + 2 * EXPERTS]
            logits = bank[:, 0:EXPERTS]
            t = now[0] + T_SEM
            m = put("vector", t, lambda e: e.tensor_reduce(best, logits, AX.X, ALU.max), [filled], "top_logit", cost=T_SMALL)
            c = put("vector", t + .2, lambda e: e.scalar_tensor_tensor(
                out=ranks, in0=logits, scalar=best, in1=tab[:, RANKS:RANKS + EXPERTS], op0=ALU.is_equal, op1=ALU.mult),
                [m, table_in], "top_ranks", cost=T_SMALL)
            f = put("vector", t + .4, lambda e: e.tensor_reduce(rank, ranks, AX.X, ALU.max), [c], "top_rank", cost=T_SMALL)
            w = put("vector", t + .6, lambda e: e.tensor_scalar(weight, ranks, rank, best, ALU.is_equal, ALU.mult), [f],
                    "top_weight", cost=T_SMALL)
            wh = stage[:, slot, 0:ER]
            weighted = drain(n, t + .8, lambda e: e.tensor_tensor(
                wh.rearrange("p (e r) -> p e r", e=EXPERTS), bank[:, EXPERTS:ROUTED].rearrange("p (e r) -> p e r", e=EXPERTS),
                weight.unsqueeze(2).to_broadcast([P, EXPERTS, RANK]), ALU.mult), [w])
            expert[half, tile] = [slot, weighted]

        def expert_turn_weighted(half, tile):
            slot, weighted = expert[half, tile]
            n, bank, filled = turn(stage[:, slot, 0:ER], P, 1, [weighted])
            stage_free[slot] = filled
            copied = drain(n, now[0] + T_SEM, lambda e: e.tensor_copy(whT[:, :], bank[:, 0:P]), [filled, whT_free[0]])
            expert[half, tile] = [slot, copied]

        def expert_out(half, tile):
            slot, copied = expert[half, tile]
            n, bank, filled = fill(4 * T_MM, lambda e, bank: e.matmul(
                bank[:, :], whT[:, :], lora_bT[:, :], start=True, stop=True), [copied, experts_ready])
            whT_free[0] = filled
            here = acc[:, tile, :]
            done = drain(n, now[0] + T_SEM, lambda e: e.scalar_tensor_tensor(
                out=here, in0=bank[:, :], scalar=gates_t[:, 1:2], in1=here, op0=ALU.mult, op1=ALU.add),
                [filled, gates_ready])
            t = now[0] + 1.0
            stored = put("sync", t, dma(out_tiles[half * HALF_TILES + tile], here), [done], f"stored{tile}", 16)
            stores.append(stored)
            if half + 1 < HALVES:
                load_acc(t + 2.5, half + 1, tile, stored)

        def load_acc(t, half, tile, free=None):
            acc_loaded[half, tile] = put("sync", t, dma(acc[:, tile, :], x_tiles[half * HALF_TILES + tile]), [free],
                                         f"acc_in{tile}", 16)

        def expert_weights():
            a_nat, r_nat, b_nat = stage[:, 0, :], stage[0:EXPERTS, 1, :], stage[:, 2, :]
            put("sync", now[0], dma(a_nat, lora_a.rearrange("e r d -> (e r) d")), [stage_free[0]], "expert_w_in", 16)
            put("sync", now[0], dma(r_nat, route_w), [stage_free[1]], "expert_w_in", 16)
            b4 = b_nat.rearrange("p (t e r) -> p t e r", t=KT, e=EXPERTS)
            for tt in range(KT):
                loaded = put("sync", now[0], dma(b4[:, tt], lora_b[:, tt * P:(tt + 1) * P, :].rearrange("e o r -> o e r")),
                             [stage_free[2]], "expert_w_in", 16)
            now[0] += 1

            def place(src, rows, dst):
                n, bank, filled = turn(src, rows, KT, [loaded])
                return drain(n, now[0] + T_SEM, lambda e: e.tensor_copy(
                    dst, bank[:, 0:KT * rows].rearrange("p (k r) -> p k r", k=KT)), [filled]), filled
            _, stage_free[0] = place(a_nat, P, routedT[:, :, EXPERTS:ROUTED])
            _, stage_free[1] = place(r_nat, EXPERTS, routedT[:, :, 0:EXPERTS])
            ready, stage_free[2] = place(b_nat, P, lora_bT[:, :].rearrange("p (k r) -> p k r", k=KT))
            return ready

        tiles = [("ctx", 0, tt) for tt in range(CHUNK_TILES)] + [("x", 0, tt) for tt in range(CHUNK_TILES)]
        pending = []

        def start_tile(item, t):
            pending.append((item, load_tile(*item, t)))

        def finish_tile():
            item, (slot, loaded) = pending.pop(0)
            turn_tile(*item, slot, loaded)

        for item in tiles[:STAGE]:
            start_tile(item, -3)
        fetch_wv(2.0, 0)
        fetch_wk(5.0, 0)
        for j in range(GROUP):
            fetch_wq(6.5 + 1.4 * j, 0, j)
        now[0] = 1.0
        for i, item in enumerate(tiles[STAGE:]):
            finish_tile()
            start_tile(item, now[0] + .1)
            now[0] += 1.0
        for tt in range(CHUNK_TILES):
            project_v(0, tt)
        project_k(0)
        later = [("ctx", 1, tt) for tt in range(CHUNK_TILES)] + [("x", 1, tt) for tt in range(CHUNK_TILES)]
        for i in range(CHUNK_TILES):
            finish_tile()
            start_tile(later.pop(0), now[0] + .1)
            now[0] += .8
        for tile in range(HALF_TILES):
            load_acc(now[0] + tile, 0, tile)
        for n in range(WO_SLOTS):
            fetch_wo(now[0] + 4 + 1.4 * n, n)
        for j in range(GROUP):
            project_q(0, j)
            finish_tile()
            if later:
                start_tile(later.pop(0), now[0] + .1)
        for _ in range(CHUNK_TILES):
            if not pending:
                break
            finish_tile()
        experts_ready = expert_weights()

        UNITS = GROUPS * CHUNKS

        def fillers_for(k):
            u, s = divmod(k, SUBS)
            lists = []
            last_units = {KV_HEADS * CHUNKS - 2: 2, KV_HEADS * CHUNKS - 1: 3}
            if u in last_units:
                index = last_units[u]
                kind = "ctx" if s == 0 else "x"
                for tt in range(CHUNK_TILES):
                    lists.append([(lambda a=(kind, index, tt): start_tile(a, now[0] - 1))])
                for tt in range(CHUNK_TILES):
                    lists[tt + 1 if tt + 1 < len(lists) else -1].append(finish_tile)
            return lists

        def expert_batches(half, c):
            steps = [expert_turn, expert_route, expert_turn_weighted, expert_out]
            batches = []
            for p in range(CHUNK_TILES + len(steps)):
                batch = []
                for i in reversed(range(len(steps))):
                    tile = p - 1 - i
                    if 0 <= tile < CHUNK_TILES:
                        batch.append(lambda f=steps[i], a=c * CHUNK_TILES + tile: f(half, a))
                if p < CHUNK_TILES:
                    batch.append(lambda a=c * CHUNK_TILES + p: expert_norm(half, a, now[0]))
                batches.append(batch)
            return batches

        small = []

        def between():
            if small:
                for step in small.pop(0):
                    step()

        for k in range(UNITS * SUBS + 1):
            u, s = divmod(k, SUBS)
            if u in (KV_HEADS * CHUNKS - 2, KV_HEADS * CHUNKS - 1):
                small.extend(fillers_for(k))
            for half in range(HALVES):
                for c in range(CHUNKS):
                    last = ((half * KV_HEADS + KV_HEADS - 1) * CHUNKS + c + 1) * SUBS
                    if k == last + 1 and k <= UNITS * SUBS:
                        small.extend(expert_batches(half, c))
            jobs = []
            nxt = u + 1
            if nxt < UNITS:
                if s == 0:
                    jobs = [lambda: project_k(nxt), lambda: project_q(nxt, 0), lambda: project_q(nxt, 1)]
                else:
                    jobs = [lambda: project_q(nxt, 2), lambda: project_q(nxt, 3)]
                if unit(nxt)[0] % 2 == 0:
                    jobs += [lambda: project_v(nxt, 2 * s), lambda: project_v(nxt, 2 * s + 1)]

            def job():
                if jobs:
                    jobs.pop(0)()
                between()

            if k < UNITS * SUBS:
                scores(k)
            job()
            between()
            if k >= 1:
                project_out(k - 1, 0)
            between()
            job()
            between()
            if k < UNITS * SUBS:
                turn_probs(k)
            if k >= 1:
                project_out(k - 1, 1)
            between()
            while jobs:
                job()
            if k < UNITS * SUBS:
                times_values(k)
            between()
        small.extend(expert_batches(HALVES - 1, CHUNKS - 1))
        while small:
            between()
            now[0] += .8
        put("sync", now[0] + 100, lambda e: e.nop(), stores)

        plan.count()
        block = stack.enter_context(nc.Block())

        @block.sync
        def _(eng):
            plan.emit("sync", eng)

        @block.tensor
        def _(eng):
            plan.emit("tensor", eng)

        @block.vector
        def _(eng):
            plan.emit("vector", eng)

        @block.scalar
        def _(eng):
            plan.emit("scalar", eng)

        @block.gpsimd
        def _(eng):
            plan.emit("gpsimd", eng)


def constants():
    half = DH // 2
    inv_freq = np.float32(1.0) / np.float32(ROPE_BASE) ** (np.arange(0, DH, 2, dtype=np.float32) / np.float32(DH))
    angle = np.arange(SEQ, dtype=np.float32)[None, :] * inv_freq.astype(np.float32)[:, None]
    table = np.zeros((P, TABLE), np.float32)
    table[:, COS:COS + SEQ] = np.concatenate([np.cos(angle), np.cos(angle)])
    table[:, SIN:SIN + SEQ] = np.concatenate([-np.sin(angle), np.sin(angle)])
    table[:, IDENT:IDENT + P] = np.eye(P, dtype=np.float32)
    table[:, RANKS:] = np.arange(EXPERTS, 0, -1, dtype=np.float32)
    return table


_INS = ['x', 'ctx_4096', 'mask_BxSxS2_ff0', 'g_xattn', 'g_ffn', 'L0_xattn_wq', 'L0_xattn_wk', 'L0_xattn_wv',
        'L0_xattn_wo', 'L0_ffn_route_w', 'L0_ffn_A', 'L0_ffn_Bw']


def kernel(**inputs):
    import concourse.bacc as bacc
    from concourse.bass_utils import run_bass_kernel_spmd

    nc = bacc.Bacc("TRN2", target_bir_lowering=False, num_devices=1)
    arrays, args = {}, []
    for name in _INS:
        a = np.ascontiguousarray(inputs[name])
        arrays[f"in_{name}"] = a
        args.append(nc.dram_tensor(f"in_{name}", a.shape, mybir.dt.from_np(a.dtype), kind="ExternalInput").ap())
    table = constants()
    arrays["table"] = table
    args.append(nc.dram_tensor("table", table.shape, F32, kind="ExternalInput").ap())
    args.append(nc.dram_tensor("out", (BATCH, SEQ, DM), F32, kind="ExternalOutput").ap())
    build(nc, *args)
    r = run_bass_kernel_spmd(nc, [arrays], core_ids=[0])
    return r.results[0]["out"]
```

```python
from contextlib import ExitStack

import numpy as np

import concourse.bass as bass
from concourse import mybir
from concourse.alu_op_type import AluOpType as ALU

F32 = mybir.dt.float32
F32R = mybir.dt.float32r
ACT = mybir.ActivationFunctionType
AX = mybir.AxisListType

P = 128
BATCH, SEQ, DM = 32, 64, 512
HEADS, KV_HEADS, DH = 32, 8, 128
EXPERTS, RANK = 8, 16
ROPE_BASE = 10000.0
LN_EPS = 1e-5

KT = DM // P
GROUP = HEADS // KV_HEADS
HALVES = 2
CHUNKS = 2
CHUNK = BATCH * SEQ // (HALVES * CHUNKS)
CHUNK_TILES = CHUNK // P
HALF_TILES = CHUNKS * CHUNK_TILES
CHUNK_SEQS = CHUNK // SEQ
SUBS = 2
SUB_SEQS = CHUNK_SEQS // SUBS
PAIRS = SUB_SEQS // 2
HEAD_PAIRS = GROUP // 2
ER = EXPERTS * RANK
ROUTED = EXPERTS + ER

GROUPS = HALVES * KV_HEADS
UNITS = GROUPS * CHUNKS
ROWS = HEAD_PAIRS * SUB_SEQS
SCALE = float(np.float32(1) / np.sqrt(np.float32(DH)))
SPLIT_PRODUCTS = ((0, 0), (0, 1), (1, 0))

TWIN_ROWS = (slice(0, SEQ), slice(SEQ, 2 * SEQ))

RAW = 4
STAGE = 4
WO_SLOTS = GROUP + 1
Q_SLOTS = 6

COS, SIN, IDENT, RANKS = 0, SEQ, 2 * SEQ, 2 * SEQ + P
TABLE = RANKS + EXPERTS


class Step:

    def __init__(self, engine, priority, emit, waits, after, signal, step, cost, size):
        self.engine, self.priority, self.emit, self.waits, self.after = engine, priority, emit, waits, after
        self.sem, self.step, self.cost, self.size = signal, step, cost, size
        self.value = None
        self.blockers, self.unblocks, self.ready = len(waits) + len(after), [], 0.0
        for w in waits + after:
            w.unblocks.append(self)


class Plan:

    def __init__(self, nc, ctx):
        self.nc, self.ctx = nc, ctx
        self.steps = []
        self.queues = {"sync": [], "tensor": [], "vector": [], "scalar": [], "gpsimd": []}
        self.sems, self.owner = {}, {}

    def put(self, engine, priority, emit, waits=(), signal=None, step=1, cost=None, after=(), size=0):
        if signal not in self.sems:
            self.sems[signal] = self.ctx.enter_context(self.nc.semaphore(signal))
            self.owner[signal] = engine
        assert self.owner[signal] == engine, signal
        s = Step(engine, (priority, len(self.steps)), emit, [w for w in waits if w is not None],
                 [w for w in after if w is not None], signal, step, COST[engine] if cost is None else cost, size)
        assert all(w.engine == engine for w in s.after)
        self.steps.append(s)
        return s

    def arrange(self):
        open_steps = {e: [] for e in self.queues}
        free = dict.fromkeys(self.queues, 0.0)
        dma_free = 0.0
        for s in self.steps:
            if not s.blockers:
                open_steps[s.engine].append(s)
        counts = dict.fromkeys(self.sems, 0)
        for _ in self.steps:
            best = None
            for engine, steps in open_steps.items():
                if steps:
                    start = max(free[engine], min(s.ready for s in steps))
                    if best is None or start < best[0]:
                        best = (start, engine)
            start, engine = best
            s = min((s for s in open_steps[engine] if s.ready <= start), key=lambda s: s.priority)
            open_steps[engine].remove(s)
            self.queues[engine].append(s)
            counts[s.sem] += s.step
            s.value = counts[s.sem]
            free[engine] = start + s.cost
            done = free[engine] + T_LATENCY[engine]
            if s.step == 16:
                dma_free = max(dma_free, start + T_DMA_START) + s.size / DMA_KB_PER_US
                done = dma_free + T_DMA_END
            s.start = start
            for t in s.unblocks:
                t.ready = max(t.ready, start if s in t.after and s not in t.waits else done)
                t.blockers -= 1
                if not t.blockers:
                    open_steps[t.engine].append(t)
        self.expected = max(free.values())

    def emit(self, engine, eng):
        passed = {}
        for s in self.queues[engine]:
            need = {}
            for w in s.waits:
                need[w.sem] = max(need.get(w.sem, 0), w.value)
            for sem, value in need.items():
                if passed.get(sem, 0) < value:
                    eng.wait_ge(self.sems[sem], value)
                    passed[sem] = value
            s.emit(eng).then_inc(self.sems[s.sem], s.step)


class Bank:

    def __init__(self, ap):
        self.ap, self.free = ap, None


COST = {"sync": .06, "vector": .6, "scalar": .52, "gpsimd": 1.2}
T_LATENCY = {"sync": .1, "vector": .15, "scalar": .2, "gpsimd": .15, "tensor": .2}
T_DMA_START, T_DMA_END, DMA_KB_PER_US = 1.4, .6, 300
T_MM = 0.2135
T_SMALL = 0.1


def build(nc, x, ctx_in, mask, g_attn, g_ffn, wq, wk, wv, wo, route_w, lora_a, lora_b, table, out):
    x_tiles = x.rearrange("b s d -> (b s) d").rearrange("(t p) d -> t p d", p=P)
    ctx_tiles = ctx_in.rearrange("b s d -> (b s) d").rearrange("(t p) d -> t p d", p=P)
    out_tiles = out.rearrange("b s d -> (b s) d").rearrange("(t p) d -> t p d", p=P)
    wq_rows = wq.rearrange("(k p) n -> p k n", p=P)
    wk_rows = wk.rearrange("(k p) n -> p k n", p=P)
    wv_rows = wv.rearrange("(k p) n -> p k n", p=P)

    stack = ExitStack()
    with stack:
        def sb(name, shape, dt=F32):
            return stack.enter_context(nc.sbuf_tensor(name, shape, dt))

        def bank(name):
            return Bank(stack.enter_context(nc.psum_tensor(name, [P, 512], F32)))

        xT = [sb(f"xT{c}", [P, 2, KT, CHUNK], F32R) for c in range(CHUNKS)]
        ctxT = [sb(f"ctxT{c}", [P, 2, KT, CHUNK], F32R) for c in range(CHUNKS)]
        wq_s = [sb(f"wq_s{j}", [P, 2, KT, DH], F32R) for j in range(GROUP)]
        wk_s = sb("wk_s", [P, 2, KT, DH], F32R)
        wv_s = sb("wv_s", [P, 2, KT, 2 * DH], F32R)
        wo_s = [sb(f"wo_s{j}", [P, 2, DM], F32R) for j in range(WO_SLOTS)]
        o_s = sb("o_s", [P, 2, PAIRS, GROUP, P], F32R)
        v_s = sb("v_s", [P, HALF_TILES, 2, 2 * DH], F32R)
        p_high = sb("p_high", [P, 2, 512], F32R)
        p_low = sb("p_low", [P, 512], F32R)
        raw = sb("raw", [P, RAW, 512])
        stage = sb("stage", [P, STAGE, DM])
        acc = sb("acc", [P, HALF_TILES, DM])
        rot = sb("rot", [P, 2, CHUNK])
        q_r = sb("q_r", [P, Q_SLOTS // 2, CHUNK_SEQS, 2, SEQ])
        k_r = sb("k_r", [P, 2, CHUNK])
        prob = sb("prob", [P, 512])
        mask_sb = sb("mask_sb", [P, CHUNKS, CHUNK_SEQS, SEQ])
        tab = sb("tab", [P, TABLE])
        routedT = sb("routedT", [P, KT, ROUTED])
        lora_bT = sb("lora_bT", [P, DM])
        gates = sb("gates", [P, 2])
        gates_t = sb("gates_t", [P, 2])
        stats = sb("stats", [P, 4, 6])
        moments = sb("moments", [P, 4, 2])
        var_eps = sb("var_eps", [P, 4])
        rstd = sb("rstd", [P, 4])
        power = sb("power", [P, 1])
        neg_max = sb("neg_max", [P, 2, ROWS])
        row_sum = sb("row_sum", [P, 2, ROWS])
        row_inv = sb("row_inv", [P, 2, ROWS])
        top = sb("top", [P, 2 + 2 * EXPERTS])
        whT = sb("whT", [P, P])

        proj = [bank("proj0"), bank("proj1")]
        small = bank("small")
        score = bank("score")
        turned = bank("turned")
        attn = [bank("attn0"), bank("attn1")]
        y = bank("y")

        plan = Plan(nc, stack)
        put = plan.put
        ident = tab[:, IDENT:IDENT + P]
        now = [0.0]

        def on_tensor(cost, emit, waits, signal, after=(), early=0.0):
            step = put("tensor", now[0] - early, emit, waits, signal, cost=cost, after=after)
            now[0] += cost
            return step

        def load(signal, dst, src, kb, waits=(), priority=None, after=()):
            return put("sync", now[0] if priority is None else priority, lambda e: e.dma_start(dst, src), waits,
                       signal, 16, after=after, size=kb)

        table_in = load("table_in", tab[:, :], table, 128, priority=-20)
        g0 = load("gates_in", gates[:, 0:1], g_attn.rearrange("(a n) -> a n", a=1).to_broadcast([P, 1]), 1, priority=15)
        gates_in = load("gates_in", gates[:, 1:2], g_ffn.rearrange("(a n) -> a n", a=1).to_broadcast([P, 1]), 1,
                        [g0], priority=15)
        gates_ready = put("scalar", 20, lambda e: e.activation(gates_t[:, :], gates[:, :], ACT.Tanh),
                          [gates_in], "gates_ready", cost=T_SMALL)
        power_set = put("gpsimd", 0, lambda e: e.memset(power[:, :], -0.5), signal="power_set", cost=T_SMALL)
        mask_in = {}

        def load_mask(index, priority, free=None):
            first = None
            for twin in range(2):
                first = load(f"mask_in{index % CHUNKS}", mask_sb[SEQ * twin:SEQ * twin + SEQ, index % CHUNKS],
                             mask[index * CHUNK_SEQS:(index + 1) * CHUNK_SEQS].rearrange("b q k -> q b k"), 128,
                             [free], priority, after=[first])
            mask_in[index] = first

        ln_done = []

        def layer_norm(src, dst, waits, priority):
            i = len(ln_done) % 4
            last = ln_done[-4] if len(ln_done) >= 4 else None
            s = put("vector", priority, lambda e: e.bn_stats(stats[:, i, :], src), waits, "ln_stats", after=[last])
            m = put("vector", priority, lambda e: e.bn_aggr(moments[:, i, :], stats[:, i, :]), [s], "ln_moments",
                    cost=T_SMALL)
            v = put("vector", priority, lambda e: e.tensor_scalar(
                var_eps[:, i:i + 1], moments[:, i, 1:2], LN_EPS, None, ALU.add), [m], "ln_var", cost=T_SMALL)
            r = put("gpsimd", priority, lambda e: e.tensor_tensor(
                rstd[:, i:i + 1], var_eps[:, i:i + 1], power[:, :], ALU.pow), [v, power_set, last], "ln_rstd", cost=.5)
            ln_done.append(put("vector", priority, lambda e: e.tensor_scalar(
                dst, src, moments[:, i, 0:1], rstd[:, i:i + 1], ALU.subtract, ALU.mult), [r], "ln_done", cost=.4))
            return ln_done[-1]

        stage_free = [None] * STAGE
        stage_count = [0]
        part_ready = {}
        chunk_free = {}

        def take_stage():
            slot = stage_count[0] % STAGE
            stage_count[0] += 1
            free = stage_free[slot]
            assert free != "taken"
            stage_free[slot] = "taken"
            return slot, free

        def turn(b, src, rows, cols, waits):
            def emit(e):
                for k in range(cols):
                    last = e.transpose(b.ap[:, k * rows:(k + 1) * rows], src[:, k * P:(k + 1) * P],
                                       ident[0:rows, 0:rows])
                return last
            return on_tensor(cols * T_MM / 2, emit, [*waits, table_in, b.free], "tile_turned")

        def prepare_tile(kind, index, tt, b, early):
            slot, free = take_stage()
            here = stage[:, slot, :]
            src = (x_tiles if kind == "x" else ctx_tiles)[index * CHUNK_TILES + tt]
            loaded = load(f"stage_in{slot}", here, src, 256, [free], now[0] - early - 3)
            if kind == "x":
                loaded = layer_norm(here, here, [loaded], now[0] - early)
            filled = turn(b, here, P, KT, [loaded])
            stage_free[slot] = filled
            dst = (xT if kind == "x" else ctxT)[index % CHUNKS]
            src = b.ap[:, :].rearrange("p (k t) -> p k t", k=KT)
            high, low = (dst[:, part, :, tt * P:(tt + 1) * P] for part in (0, 1))
            h = put("scalar", now[0], lambda e: e.activation(high, src, ACT.Copy),
                    [filled, *chunk_free.get((kind, index % CHUNKS), [])], "tile_high")
            b.free = put("vector", now[0], lambda e: e.tensor_tensor(low, src, high.bitcast(F32), ALU.subtract), [h],
                         "tile_low")
            part_ready.setdefault((kind, index), []).append(b.free)

        raw_free = [None] * RAW
        raw_count = [0]

        def fetch(priority, src, k, high, low, free):
            slot = raw_count[0] % RAW
            raw_count[0] += 1
            here = raw[:, slot, :] if k == 1 else raw[:, slot, :].rearrange("p (k n) -> p k n", k=k)
            loaded = load(f"raw_in{slot}", here, src, 256, [raw_free[slot]], priority - 4)
            h = put("scalar", priority, lambda e: e.activation(high, here, ACT.Copy), [loaded, free], "weight_high")
            engine = "vector" if k == 1 else "gpsimd"
            raw_free[slot] = put(engine, priority, lambda e: e.tensor_tensor(low, here, high.bitcast(F32), ALU.subtract),
                                 [h], f"weight_low_{engine}")
            return raw_free[slot]

        wq_ready, wk_ready, wv_ready, wo_ready = {}, {}, {}, {}

        def fetch_wq(priority, G, j, free=None):
            col = ((G % KV_HEADS) * GROUP + j) * DH
            wq_ready[G, j] = fetch(priority, wq_rows[:, :, col:col + DH], KT, wq_s[j][:, 0], wq_s[j][:, 1], free)

        def fetch_wk(priority, G, free=None):
            col = (G % KV_HEADS) * DH
            wk_ready[G] = fetch(priority, wk_rows[:, :, col:col + DH], KT, wk_s[:, 0], wk_s[:, 1], free)

        def fetch_wv(priority, G, free=None):
            col = (G % KV_HEADS) * DH
            wv_ready[G] = [fetch(priority, wv_rows[:, k:k + 2, col:col + 2 * DH], 2, wv_s[:, 0, k:k + 2],
                                 wv_s[:, 1, k:k + 2], free) for k in range(0, KT, 2)]

        def fetch_wo(priority, n, free=None):
            row = (n % HEADS) * DH
            w = wo_s[n % WO_SLOTS]
            wo_ready[n] = fetch(priority, wo[row:row + DH, :], 1, w[:, 0], w[:, 1], free)

        def unit(u):
            G, c = divmod(u, CHUNKS)
            return G, c, (G // KV_HEADS) * CHUNKS + c

        proj_count = [0]

        def project(width, stationary, moving, waits):
            b = proj[proj_count[0] % 2]
            proj_count[0] += 1

            def emit(e):
                for k in range(KT):
                    for i, (s, m) in enumerate(SPLIT_PRODUCTS):
                        last = e.matmul(b.ap[:, 0:width], stationary(s, k), moving(m, k), start=(k == 0 and i == 0),
                                        stop=(k == KT - 1 and i == 2))
                return last
            return b, on_tensor(3 * KT * T_MM * width / 512, emit, [*waits, b.free], "projected")

        rope_added = []
        roped = {}
        scored = {}
        values_used = {}

        def rope(b, filled, dst, dst_free):
            i = len(rope_added)
            r = rot[:, i % 2, :]
            free = rope_added[i - 2] if i >= 2 else None
            half = DH // 2
            per_seq = [P, CHUNK_SEQS, SEQ]
            cos = tab[:, COS:COS + SEQ].unsqueeze(1).to_broadcast(per_seq)
            sin = tab[:, SIN:SIN + SEQ].unsqueeze(1).to_broadcast(per_seq)
            src, r3 = (v.rearrange("p (b s) -> p b s", s=SEQ) for v in (b.ap[:, :], r))

            def shift(e):
                e.activation(r[0:half, :], b.ap[half:DH, :], ACT.Copy)
                return e.activation(r[half:DH, :], b.ap[0:half, :], ACT.Copy)
            a = put("scalar", now[0], shift, [filled, free], "shifted_half", cost=1.0)
            s = put("gpsimd", now[0], lambda e: e.tensor_tensor(r3, r3, sin, ALU.mult), [a, table_in], "times_sin")
            c = put("vector", now[0], lambda e: e.tensor_tensor(dst, src, cos, ALU.mult), [a, dst_free, table_in],
                    "times_cos")
            b.free = c
            done = put("vector", now[0], lambda e: e.tensor_tensor(dst, dst, r3, ALU.add), [s, c], "rope_added")
            rope_added.append(done)
            return done

        def project_k(u):
            G, c, index = unit(u)
            b, filled = project(CHUNK, lambda s, k: wk_s[:, s, k, :], lambda m, k: ctxT[c][:, m, k, :],
                                [wk_ready[G], *part_ready["ctx", index]])
            roped[u, "k"] = rope(b, filled, k_r[:, u % 2, :].rearrange("p (b s) -> p b s", s=SEQ),
                                 scored.get(SUBS * (u - 2) + 1))
            chunk_free["ctx", c] = chunk_free.get(("ctx", c), [])[-CHUNK_TILES:] + [filled]
            if c == CHUNKS - 1 and G + 1 < GROUPS:
                fetch_wk(now[0] + 12, G + 1, filled)

        def project_q(u, j):
            G, c, index = unit(u)
            n = GROUP * u + j
            free = scored.get(SUBS * ((n - Q_SLOTS) // GROUP) + 1)
            b, filled = project(CHUNK, lambda s, k: wq_s[j][:, s, k, :], lambda m, k: xT[c][:, m, k, :],
                                [wq_ready[G, j], *part_ready["x", index]])
            roped[u, j] = rope(b, filled, q_r[:, n % Q_SLOTS // 2, :, n % 2, :], free)
            chunk_free["x", c] = chunk_free.get(("x", c), [])[-GROUP:] + [filled]
            if c == CHUNKS - 1 and G + 1 < GROUPS:
                fetch_wq(now[0] + 12, G + 1, j, filled)

        v_ready = {}

        def project_v(u, tt):
            G, c, index = unit(u)
            tile = c * CHUNK_TILES + tt
            b, filled = project(2 * DH, lambda s, k: ctxT[c][:, s, k, tt * P:(tt + 1) * P], lambda m, k: wv_s[:, m, k, :],
                                [*wv_ready[G], *part_ready["ctx", index]])
            chunk_free["ctx", c] = chunk_free.get(("ctx", c), [])[-CHUNK_TILES:] + [filled]
            h, low = None, None
            for twin, (own, other) in enumerate((TWIN_ROWS, TWIN_ROWS[::-1])):
                src, high = b.ap[own, 0:2 * DH], v_s[own, tile, twin, :]
                h = put("scalar", now[0], lambda e, high=high, src=src: e.activation(high, src, ACT.Copy),
                        [filled, values_used.get(SUBS * (u - 2) + 1)], "v_high", cost=.3, after=[h])
                low = put("vector", now[0], lambda e, high=high, src=src, dst=v_s[other, tile, twin, :]:
                          e.tensor_tensor(dst, src, high.bitcast(F32), ALU.subtract), [h], "v_low", cost=.35, after=[low])
            b.free = v_ready[G // 2, tile] = low
            if c == CHUNKS - 1 and tt == CHUNK_TILES - 1 and G + 2 < GROUPS:
                fetch_wv(now[0] + 35, G + 2, filled)

        normalised, probs_turned, probs_split, low_made = {}, {}, {}, {}
        out_used = {}
        acc_loaded, x1_ready = {}, {}

        def scores(k):
            u, s = divmod(k, SUBS)
            G, c, index = unit(u)

            def emit(e):
                for hp in range(HEAD_PAIRS):
                    for b in range(SUB_SEQS):
                        seq = s * SUB_SEQS + b
                        col = (hp * SUB_SEQS + b) * SEQ
                        two_heads = q_r[:, (GROUP * u + 2 * hp) % Q_SLOTS // 2, seq, :, :].rearrange("p h s -> p (h s)")
                        last = e.matmul(score.ap[:, col:col + SEQ], two_heads, k_r[:, u % 2, seq * SEQ:(seq + 1) * SEQ],
                                        start=True, stop=True)
                return last
            scored[k] = on_tensor(1.65, emit, [roped[u, w] for w in ("k", *range(GROUP))] + [score.free], "scored")
            i = k % 2
            p = prob[:, :]
            by_head = p.rearrange("p (h n) -> p h n", h=HEAD_PAIRS)
            by_row = p.rearrange("p (r k) -> p r k", r=ROWS)
            m = mask_sb[:, c, s * SUB_SEQS:(s + 1) * SUB_SEQS, :].rearrange("p b k -> p (b k)").unsqueeze(1).to_broadcast(
                [P, HEAD_PAIRS, SUB_SEQS * SEQ])
            masked = put("vector", now[0], lambda e: e.scalar_tensor_tensor(
                out=by_head, in0=score.ap[:, :].rearrange("p (h n) -> p h n", h=HEAD_PAIRS), scalar=SCALE, in1=m,
                op0=ALU.mult, op1=ALU.add), [scored[k], mask_in[index], probs_turned.get(k - 1)], "masked")
            score.free = masked
            if s == SUBS - 1 and G == KV_HEADS - 1:
                load_mask(index + CHUNKS, now[0] + 5, masked)
            a = put("vector", now[0], lambda e: e.tensor_reduce(neg_max[:, i, :], by_row, AX.X, ALU.max, negate=True),
                    [masked], "neg_max")
            b = put("gpsimd", now[0], lambda e: e.tensor_tensor(
                by_row, by_row, neg_max[:, i, :].unsqueeze(2).to_broadcast([P, ROWS, SEQ]), ALU.add), [a], "less_max")
            ex = put("scalar", now[0], lambda e: e.activation(p, p, ACT.Exp), [b], "exponentials")
            sm = put("vector", now[0], lambda e: e.tensor_reduce(row_sum[:, i, :], by_row, AX.X, ALU.add), [ex], "row_sum")
            inv = put("vector", now[0], lambda e: e.reciprocal(row_inv[:, i, :], row_sum[:, i, :]), [sm], "row_inv",
                      cost=T_SMALL)
            normalised[k] = put("gpsimd", now[0], lambda e: e.tensor_tensor(
                by_row, by_row, row_inv[:, i, :].unsqueeze(2).to_broadcast([P, ROWS, SEQ]), ALU.mult), [inv], "normalised")

        def turn_probs(k):
            def emit(e):
                for bp in range(PAIRS):
                    for hp in range(HEAD_PAIRS):
                        src = (hp * PAIRS + bp) * P
                        dst = (bp * HEAD_PAIRS + hp) * P
                        last = e.transpose(turned.ap[:, dst:dst + P], prob[:, src:src + P], ident)
                return last
            probs_turned[k] = on_tensor(.43, emit, [normalised[k], turned.free], "probs_turned")
            h, low = None, None
            for twin, rows in enumerate(TWIN_ROWS):
                src = turned.ap[rows, :]

                def twice(e, src=src, twin=twin):
                    e.activation(p_high[TWIN_ROWS[1 - twin], twin, :], src, ACT.Copy)
                    return e.activation(p_high[TWIN_ROWS[twin], twin, :], src, ACT.Copy)
                h = put("scalar", now[0], twice, [probs_turned[k], values_used.get(k - 1)], "probs_high", cost=1.0,
                        after=[h])
                low = put("vector", now[0], lambda e, rows=rows, src=src, twin=twin: e.tensor_tensor(
                    p_low[rows, :], src, p_high[rows, twin, :].bitcast(F32), ALU.subtract),
                    [h, values_used.get(k - 1)], "probs_low", after=[low])
            turned.free = probs_split[k] = low

        def times_values(k):
            u, s = divmod(k, SUBS)
            G, c, index = unit(u)
            tiles = [c * CHUNK_TILES + s * PAIRS + bp for bp in range(PAIRS)]
            head = slice((G % 2) * DH, (G % 2 + 1) * DH)

            def highs(e):
                for bp in range(PAIRS):
                    cols = slice(bp * GROUP * SEQ, (bp + 1) * GROUP * SEQ)
                    for twin in range(2):
                        last = e.matmul(attn[twin].ap[:, cols], v_s[:, tiles[bp], twin, head], p_high[:, twin, cols],
                                        start=(bp == 0), stop=False, skip_group_check=True)
                return last

            def lows(e):
                for bp in range(PAIRS):
                    cols = slice(bp * GROUP * SEQ, (bp + 1) * GROUP * SEQ)
                    for twin, rows in enumerate(TWIN_ROWS):
                        last = e.matmul(attn[twin].ap[:, cols], v_s[rows, tiles[bp], twin, head], p_low[rows, cols],
                                        start=False, stop=True, skip_group_check=True)
                return last
            first = on_tensor(2 * T_MM, highs, [probs_split[k], attn[0].free, attn[1].free] +
                              [v_ready[G // 2, t] for t in tiles], "values_times_high")
            values_used[k] = on_tensor(2 * T_MM, lows, [], "values_used", after=[first])
            for twin in range(2):
                src = attn[twin].ap[:, :].rearrange("p (b h q) -> p b h q", b=PAIRS, h=GROUP)
                high, low = (o_s[:, part, :, :, SEQ * twin:SEQ * twin + SEQ] for part in (0, 1))
                h = put("scalar", now[0], lambda e, high=high, src=src: e.activation(high, src, ACT.Copy),
                        [values_used[k], out_used.get(k - 1)], "out_high")
                attn[twin].free = low_made[k, twin] = put(
                    "vector", now[0], lambda e, high=high, low=low, src=src:
                    e.tensor_tensor(low, src, high.bitcast(F32), ALU.subtract), [h], "out_low")

        def project_out(k, bp):
            u, s = divmod(k, SUBS)
            G, c, index = unit(u)
            last_use = c == CHUNKS - 1 and s == SUBS - 1 and bp == PAIRS - 1
            used = None
            for h in range(GROUP):
                n = G * GROUP + h
                w = wo_s[n % WO_SLOTS]

                def emit(e, h=h, w=w):
                    for i, (a, b) in enumerate(SPLIT_PRODUCTS):
                        last = e.matmul(y.ap[:, :], o_s[:, a, bp, h, :], w[:, b, :], start=(h == 0 and i == 0),
                                        stop=(h == GROUP - 1 and i == 2))
                    return last
                used = on_tensor(3 * T_MM, emit, [wo_ready[n], low_made[k, 0], low_made[k, 1], y.free], "out_projected",
                                 after=[used])
                if last_use and n + WO_SLOTS < GROUPS * GROUP:
                    fetch_wo(now[0], n + WO_SLOTS, used)
            out_used[k] = used
            tile = c * CHUNK_TILES + s * PAIRS + bp
            half = G // KV_HEADS
            here = acc[:, tile, :]
            y.free = x1_ready[half, tile] = put("vector", now[0], lambda e: e.scalar_tensor_tensor(
                out=here, in0=y.ap[:, :], scalar=gates_t[:, 0:1], in1=here, op0=ALU.mult, op1=ALU.add),
                [used, gates_ready, acc_loaded[half, tile], x1_ready.get((half, tile))], "x1_added")

        whT_free = [None]
        stores = []

        def experts(half, tile, b):
            here = acc[:, tile, :]
            slot, free = take_stage()
            at = stage[:, slot, :]
            normed = layer_norm(here, at, [x1_ready[half, tile], free], now[0])
            t = turn(b, at, P, KT, [normed])
            b.free = copied = put("vector", now[0], lambda e: e.tensor_copy(at, b.ap[:, :]), [t], "x1_turned")

            def route(e):
                for k in range(KT):
                    last = e.matmul(b.ap[:, 0:ROUTED], at[:, k * P:(k + 1) * P], routedT[:, k, :], start=(k == 0),
                                    stop=(k == KT - 1))
                return last
            routed = on_tensor(KT * 4 * ROUTED / 2400, route, [copied, experts_ready, b.free], "routed")
            best, rank, ranks, weight = top[:, 0:1], top[:, 1:2], top[:, 2:2 + EXPERTS], top[:, 2 + EXPERTS:]
            logits = b.ap[:, 0:EXPERTS]
            small_step = {"cost": T_SMALL}
            m = put("vector", now[0], lambda e: e.tensor_reduce(best, logits, AX.X, ALU.max), [routed], "top_logit",
                    after=top_free, **small_step)
            r = put("vector", now[0], lambda e: e.scalar_tensor_tensor(
                out=ranks, in0=logits, scalar=best, in1=tab[:, RANKS:RANKS + EXPERTS], op0=ALU.is_equal, op1=ALU.mult),
                [m, table_in], "top_ranks", **small_step)
            f = put("vector", now[0], lambda e: e.tensor_reduce(rank, ranks, AX.X, ALU.max), [r], "top_rank", **small_step)
            w = put("vector", now[0], lambda e: e.tensor_scalar(weight, ranks, rank, best, ALU.is_equal, ALU.mult), [f],
                    "top_weight", **small_step)
            wh = at[:, 0:ER]
            by_expert = "p (e r) -> p e r"
            b.free = weighted = put("vector", now[0], lambda e: e.tensor_tensor(
                wh.rearrange(by_expert, e=EXPERTS), b.ap[:, EXPERTS:ROUTED].rearrange(by_expert, e=EXPERTS),
                weight.unsqueeze(2).to_broadcast([P, EXPERTS, RANK]), ALU.mult), [w], "weighted", cost=.25)
            top_free[:] = [weighted]
            stage_free[slot] = t = turn(b, wh, P, 1, [weighted])
            b.free = copied = put("vector", now[0], lambda e: e.tensor_copy(whT[:, :], b.ap[:, 0:P]), [t, whT_free[0]],
                                  "weighted_turned", cost=.25)
            whT_free[0] = mixed = on_tensor(4 * T_MM, lambda e: e.matmul(
                b.ap[:, :], whT[:, :], lora_bT[:, :], start=True, stop=True), [copied, experts_ready, b.free], "mixed")
            b.free = done = put("vector", now[0], lambda e: e.scalar_tensor_tensor(
                out=here, in0=b.ap[:, :], scalar=gates_t[:, 1:2], in1=here, op0=ALU.mult, op1=ALU.add),
                [mixed, gates_ready], "out_ready")
            stored = load(f"stored{tile}", out_tiles[half * HALF_TILES + tile], here, 256, [done])
            stores.append(stored)
            if half + 1 < HALVES:
                load_acc(half + 1, tile, stored)

        top_free = []

        def load_acc(half, tile, free=None):
            acc_loaded[half, tile] = load(f"acc_in{tile}", acc[:, tile, :], x_tiles[half * HALF_TILES + tile], 256, [free])

        def expert_weights():
            (sa, free_a), (sr, free_r), (sbw, free_b) = take_stage(), take_stage(), take_stage()
            a_nat, r_nat, b_nat = stage[:, sa, :], stage[0:EXPERTS, sr, :], stage[:, sbw, :]
            a_in = load("lora_a_in", a_nat, lora_a.rearrange("e r d -> (e r) d"), 256, [free_a])
            r_in = load("route_w_in", r_nat, route_w, 16, [free_r])
            b4 = b_nat.rearrange("p (t e r) -> p t e r", t=KT, e=EXPERTS)
            b_in = None
            for tt in range(KT):
                b_in = load("lora_b_in", b4[:, tt], lora_b[:, tt * P:(tt + 1) * P, :].rearrange("e o r -> o e r"), 128,
                            [free_b], after=[b_in])

            def place(src, rows, dst, arrived):
                t = turn(small, src, rows, KT, [arrived])
                small.free = put("vector", now[0], lambda e: e.tensor_copy(
                    dst, small.ap[:, 0:KT * rows].rearrange("p (k r) -> p k r", k=KT)), [t], "expert_weights")
                return t
            stage_free[sa] = place(a_nat, P, routedT[:, :, EXPERTS:ROUTED], a_in)
            stage_free[sr] = place(r_nat, EXPERTS, routedT[:, :, 0:EXPERTS], r_in)
            stage_free[sbw] = place(b_nat, P, lora_bT[:, :].rearrange("p (k r) -> p k r", k=KT), b_in)
            return small.free

        prologue_banks = [small, score, turned, y]

        def prepare_chunk(index, kinds, banks, early):
            for i, (kind, tt) in enumerate((kind, tt) for kind in kinds for tt in range(CHUNK_TILES)):
                prepare_tile(kind, index, tt, banks[i % len(banks)], early)

        prepare_chunk(0, ["ctx"], prologue_banks, 10)
        fetch_wk(-2, 0)
        fetch_wv(-1, 0)
        prepare_chunk(0, ["x"], prologue_banks, 10)
        for j in range(GROUP):
            fetch_wq(1 + j, 0, j)
        project_k(0)
        for tt in range(CHUNK_TILES):
            project_v(0, tt)
        load_mask(0, 10)
        load_mask(1, 30)
        for j in range(GROUP):
            project_q(0, j)
        prepare_chunk(1, ["ctx", "x"], [small, turned], 12)
        for n in range(WO_SLOTS):
            fetch_wo(now[0] + n, n)
        for tile in range(HALF_TILES):
            load_acc(0, tile)

        for k in range(UNITS * SUBS + 1):
            u, s = divmod(k, SUBS)
            jobs = []
            nxt = u + 1
            if nxt < UNITS:
                if s == 0:
                    jobs = [lambda: project_k(nxt), lambda: project_q(nxt, 0), lambda: project_q(nxt, 1)]
                else:
                    jobs = [lambda: project_q(nxt, 2), lambda: project_q(nxt, 3)]
                if unit(nxt)[0] % 2 == 0:
                    jobs += [lambda: project_v(nxt, 2 * s), lambda: project_v(nxt, 2 * s + 1)]

            def job():
                if jobs:
                    jobs.pop(0)()

            if k < UNITS * SUBS:
                scores(k)
            job()
            if k >= 1:
                project_out(k - 1, 0)
            job()
            if k < UNITS * SUBS:
                turn_probs(k)
            if k >= 1:
                project_out(k - 1, 1)
            while jobs:
                job()
            if k < UNITS * SUBS:
                times_values(k)
            if k == 1:
                experts_ready = expert_weights()
            if u in (KV_HEADS * CHUNKS - 2, KV_HEADS * CHUNKS - 1):
                prepare_chunk(u - KV_HEADS * CHUNKS + 4, ["ctx" if s == 0 else "x"], [small], 12)
            for half in range(HALVES):
                for c in range(CHUNKS):
                    done = ((half * KV_HEADS + KV_HEADS - 1) * CHUNKS + c) * SUBS
                    if k - 1 - done in (0, 1):
                        for bp in range(PAIRS):
                            tail = half == HALVES - 1 and c == CHUNKS - 1
                            experts(half, c * CHUNK_TILES + (k - 1 - done) * PAIRS + bp, proj[bp] if tail else small)

        last_stores = put("sync", now[0] + 1e6, lambda e: e.nop(), stores, "all_stored")
        plan.arrange()
        block = stack.enter_context(nc.Block())

        @block.sync
        def _(eng):
            plan.emit("sync", eng)

        @block.tensor
        def _(eng):
            plan.emit("tensor", eng)

        @block.vector
        def _(eng):
            plan.emit("vector", eng)

        @block.scalar
        def _(eng):
            plan.emit("scalar", eng)

        @block.gpsimd
        def _(eng):
            plan.emit("gpsimd", eng)


def constants():
    half = DH // 2
    inv_freq = np.float32(1.0) / np.float32(ROPE_BASE) ** (np.arange(0, DH, 2, dtype=np.float32) / np.float32(DH))
    angle = np.arange(SEQ, dtype=np.float32)[None, :] * inv_freq.astype(np.float32)[:, None]
    table = np.zeros((P, TABLE), np.float32)
    table[:, COS:COS + SEQ] = np.concatenate([np.cos(angle), np.cos(angle)])
    table[:, SIN:SIN + SEQ] = np.concatenate([-np.sin(angle), np.sin(angle)])
    table[:, IDENT:IDENT + P] = np.eye(P, dtype=np.float32)
    table[:, RANKS:] = np.arange(EXPERTS, 0, -1, dtype=np.float32)
    return table


_INS = ['x', 'ctx_4096', 'mask_BxSxS2_ff0', 'g_xattn', 'g_ffn', 'L0_xattn_wq', 'L0_xattn_wk', 'L0_xattn_wv',
        'L0_xattn_wo', 'L0_ffn_route_w', 'L0_ffn_A', 'L0_ffn_Bw']


def kernel(**inputs):
    import concourse.bacc as bacc
    from concourse.bass_utils import run_bass_kernel_spmd

    nc = bacc.Bacc("TRN2", target_bir_lowering=False, num_devices=1)
    arrays, args = {}, []
    for name in _INS:
        a = np.ascontiguousarray(inputs[name])
        arrays[f"in_{name}"] = a
        args.append(nc.dram_tensor(f"in_{name}", a.shape, mybir.dt.from_np(a.dtype), kind="ExternalInput").ap())
    table = constants()
    arrays["table"] = table
    args.append(nc.dram_tensor("table", table.shape, F32, kind="ExternalInput").ap())
    args.append(nc.dram_tensor("out", (BATCH, SEQ, DM), F32, kind="ExternalOutput").ap())
    build(nc, *args)
    r = run_bass_kernel_spmd(nc, [arrays], core_ids=[0])
    return r.results[0]["out"]
```

```python
from contextlib import ExitStack

import numpy as np

import concourse.bass as bass
from concourse import mybir
from concourse.alu_op_type import AluOpType as ALU

F32 = mybir.dt.float32
F32R = mybir.dt.float32r
ACT = mybir.ActivationFunctionType
AX = mybir.AxisListType

P = 128
BATCH, SEQ, DM = 32, 64, 512
HEADS, KV_HEADS, DH = 32, 8, 128
EXPERTS, RANK = 8, 16
ROPE_BASE = 10000.0
LN_EPS = 1e-5

KT = DM // P
GROUP = HEADS // KV_HEADS
HALVES = 2
CHUNKS = 2
CHUNK = BATCH * SEQ // (HALVES * CHUNKS)
CHUNK_TILES = CHUNK // P
HALF_TILES = CHUNKS * CHUNK_TILES
CHUNK_SEQS = CHUNK // SEQ
SUBS = 2
SUB_SEQS = CHUNK_SEQS // SUBS
PAIRS = SUB_SEQS // 2
HEAD_PAIRS = GROUP // 2
ER = EXPERTS * RANK
ROUTED = EXPERTS + ER

GROUPS = HALVES * KV_HEADS
UNITS = GROUPS * CHUNKS
ROWS = HEAD_PAIRS * SUB_SEQS
SCALE = float(np.float32(1) / np.sqrt(np.float32(DH)))
SPLIT_PRODUCTS = ((0, 0), (0, 1), (1, 0))

TWIN_ROWS = (slice(0, SEQ), slice(SEQ, 2 * SEQ))

RAW = 4
STAGE = 4
UNSHARED_CHUNKS = CHUNKS + 1
ANY_SLOT, TOKEN_SLOTS, EXPERT_SLOTS = (0, 1, 2, 3), (0, 1), (2, 3)
WO_SLOTS = GROUP + 1
Q_SLOTS = 6

COS, SIN, IDENT, RANKS = 0, SEQ, 2 * SEQ, 2 * SEQ + P
TABLE = RANKS + EXPERTS


class Step:

    def __init__(self, engine, priority, emit, waits, after, signal, step, cost, size):
        self.engine, self.priority, self.emit, self.waits, self.after = engine, priority, emit, waits, after
        self.sem, self.step, self.cost, self.size = signal, step, cost, size
        self.value = None
        self.blockers, self.unblocks, self.ready = len(waits) + len(after), [], 0.0
        for w in waits + after:
            w.unblocks.append(self)


class Plan:

    def __init__(self, nc, ctx):
        self.nc, self.ctx = nc, ctx
        self.steps = []
        self.queues = {"sync": [], "tensor": [], "vector": [], "scalar": [], "gpsimd": []}
        self.sems, self.owner = {}, {}

    def put(self, engine, priority, emit, waits=(), signal=None, step=1, cost=None, after=(), size=0):
        if signal not in self.sems:
            self.sems[signal] = self.ctx.enter_context(self.nc.semaphore(signal))
            self.owner[signal] = engine
        assert self.owner[signal] == engine, signal
        s = Step(engine, (priority, len(self.steps)), emit, [w for w in waits if w is not None],
                 [w for w in after if w is not None], signal, step, COST[engine] if cost is None else cost, size)
        assert all(w.engine == engine for w in s.after)
        self.steps.append(s)
        return s

    def arrange(self):
        open_steps = {e: [] for e in self.queues}
        free = dict.fromkeys(self.queues, 0.0)
        dma_free = 0.0
        for s in self.steps:
            if not s.blockers:
                open_steps[s.engine].append(s)
        counts = dict.fromkeys(self.sems, 0)
        for _ in self.steps:
            best = None
            for engine, steps in open_steps.items():
                if steps:
                    start = max(free[engine], min(s.ready for s in steps))
                    if best is None or start < best[0]:
                        best = (start, engine)
            start, engine = best
            s = min((s for s in open_steps[engine] if s.ready <= start), key=lambda s: s.priority)
            open_steps[engine].remove(s)
            self.queues[engine].append(s)
            counts[s.sem] += s.step
            s.value = counts[s.sem]
            free[engine] = start + s.cost
            done = free[engine] + T_LATENCY[engine]
            if s.step == 16:
                dma_free = max(dma_free, start + T_DMA_START) + s.size / DMA_KB_PER_US
                done = dma_free + T_DMA_END
            s.start = start
            for t in s.unblocks:
                t.ready = max(t.ready, start if s in t.after and s not in t.waits else done)
                t.blockers -= 1
                if not t.blockers:
                    open_steps[t.engine].append(t)
        self.expected = max(free.values())

    def emit(self, engine, eng):
        passed = {}
        for s in self.queues[engine]:
            need = {}
            for w in s.waits:
                need[w.sem] = max(need.get(w.sem, 0), w.value)
            for sem, value in need.items():
                if passed.get(sem, 0) < value:
                    eng.wait_ge(self.sems[sem], value)
                    passed[sem] = value
            s.emit(eng).then_inc(self.sems[s.sem], s.step)


class Bank:

    def __init__(self, ap):
        self.ap, self.free = ap, None


COST = {"sync": .06, "vector": .6, "scalar": .52, "gpsimd": 1.2}
T_LATENCY = {"sync": .1, "vector": .15, "scalar": .2, "gpsimd": .15, "tensor": .2}
T_DMA_START, T_DMA_END, DMA_KB_PER_US = 1.4, .6, 300
T_MM = 0.2135
T_SMALL = 0.1
EXPERT_DELAY = ((8, 25, 12, 0), (0, 14, 20, 0))


def build(nc, x, ctx_in, mask, g_attn, g_ffn, wq, wk, wv, wo, route_w, lora_a, lora_b, table, out):
    x_tiles = x.rearrange("b s d -> (b s) d").rearrange("(t p) d -> t p d", p=P)
    ctx_tiles = ctx_in.rearrange("b s d -> (b s) d").rearrange("(t p) d -> t p d", p=P)
    out_tiles = out.rearrange("b s d -> (b s) d").rearrange("(t p) d -> t p d", p=P)
    wq_rows = wq.rearrange("(k p) n -> p k n", p=P)
    wk_rows = wk.rearrange("(k p) n -> p k n", p=P)
    wv_rows = wv.rearrange("(k p) n -> p k n", p=P)

    stack = ExitStack()
    with stack:
        def sb(name, shape, dt=F32):
            return stack.enter_context(nc.sbuf_tensor(name, shape, dt))

        def bank(name):
            return Bank(stack.enter_context(nc.psum_tensor(name, [P, 512], F32)))

        xT = [sb(f"xT{c}", [P, 2, KT, CHUNK], F32R) for c in range(CHUNKS)]
        ctxT = [sb(f"ctxT{c}", [P, 2, KT, CHUNK], F32R) for c in range(CHUNKS)]
        wq_s = [sb(f"wq_s{j}", [P, 2, KT, DH], F32R) for j in range(GROUP)]
        wk_s = sb("wk_s", [P, 2, KT, DH], F32R)
        wv_s = sb("wv_s", [P, 2, KT, 2 * DH], F32R)
        wo_s = [sb(f"wo_s{j}", [P, 2, DM], F32R) for j in range(WO_SLOTS)]
        o_s = sb("o_s", [P, 2, PAIRS, GROUP, P], F32R)
        v_s = sb("v_s", [P, HALF_TILES, 2, 2 * DH], F32R)
        p_high = sb("p_high", [P, 2, 512], F32R)
        p_low = sb("p_low", [P, 512], F32R)
        raw = sb("raw", [P, RAW, 512])
        stage = sb("stage", [P, STAGE, DM])
        acc = sb("acc", [P, HALF_TILES, DM])
        rot = sb("rot", [P, 2, CHUNK])
        q_r = sb("q_r", [P, Q_SLOTS // 2, CHUNK_SEQS, 2, SEQ])
        k_r = sb("k_r", [P, 2, CHUNK])
        prob = sb("prob", [P, 512])
        mask_sb = sb("mask_sb", [P, CHUNKS, CHUNK_SEQS, SEQ])
        tab = sb("tab", [P, TABLE])
        routedT = sb("routedT", [P, KT, ROUTED])
        lora_bT = sb("lora_bT", [P, DM])
        gates = sb("gates", [P, 2])
        gates_t = sb("gates_t", [P, 2])
        stats = sb("stats", [P, 4, 6])
        moments = sb("moments", [P, 4, 2])
        var_eps = sb("var_eps", [P, 4])
        rstd = sb("rstd", [P, 4])
        power = sb("power", [P, 1])
        neg_max = sb("neg_max", [P, 2, ROWS])
        row_sum = sb("row_sum", [P, 2, ROWS])
        row_inv = sb("row_inv", [P, 2, ROWS])
        top = sb("top", [P, STAGE, 2 + 2 * EXPERTS])

        proj = [bank("proj0"), bank("proj1")]
        small = bank("small")
        score = bank("score")
        turned = bank("turned")
        attn = [bank("attn0"), bank("attn1")]
        y = bank("y")

        plan = Plan(nc, stack)
        put = plan.put
        ident = tab[:, IDENT:IDENT + P]
        now = [0.0]

        def on_tensor(cost, emit, waits, signal, after=(), priority=None):
            step = put("tensor", now[0] if priority is None else priority, emit, waits, signal, cost=cost, after=after)
            now[0] += cost
            return step

        def load(signal, dst, src, kb, waits=(), priority=None, after=()):
            return put("sync", now[0] if priority is None else priority, lambda e: e.dma_start(dst, src), waits,
                       signal, 16, after=after, size=kb)

        table_in = load("table_in", tab[:, :], table, 128, priority=-20)
        g0 = load("gates_in", gates[:, 0:1], g_attn.rearrange("(a n) -> a n", a=1).to_broadcast([P, 1]), 1, priority=15)
        gates_in = load("gates_in", gates[:, 1:2], g_ffn.rearrange("(a n) -> a n", a=1).to_broadcast([P, 1]), 1,
                        [g0], priority=15)
        gates_ready = put("scalar", 20, lambda e: e.activation(gates_t[:, :], gates[:, :], ACT.Tanh),
                          [gates_in], "gates_ready", cost=T_SMALL)
        power_set = put("gpsimd", 0, lambda e: e.memset(power[:, :], -0.5), signal="power_set", cost=T_SMALL)
        mask_in = {}

        def load_mask(index, priority, free=None):
            first = None
            for twin in range(2):
                first = load(f"mask_in{index % CHUNKS}", mask_sb[SEQ * twin:SEQ * twin + SEQ, index % CHUNKS],
                             mask[index * CHUNK_SEQS:(index + 1) * CHUNK_SEQS].rearrange("b q k -> q b k"), 128,
                             [free], priority, after=[first])
            mask_in[index] = first

        ln_done = []

        def layer_norm(src, dst, waits, priority):
            i = len(ln_done) % 4
            last = ln_done[-4] if len(ln_done) >= 4 else None
            s = put("vector", priority, lambda e: e.bn_stats(stats[:, i, :], src), waits, "ln_stats", after=[last])
            m = put("vector", priority, lambda e: e.bn_aggr(moments[:, i, :], stats[:, i, :]), [s], "ln_moments",
                    cost=T_SMALL)
            v = put("vector", priority, lambda e: e.tensor_scalar(
                var_eps[:, i:i + 1], moments[:, i, 1:2], LN_EPS, None, ALU.add), [m], "ln_var", cost=T_SMALL)
            r = put("gpsimd", priority, lambda e: e.tensor_tensor(
                rstd[:, i:i + 1], var_eps[:, i:i + 1], power[:, :], ALU.pow), [v, power_set, last], "ln_rstd", cost=.5)
            ln_done.append(put("vector", priority, lambda e: e.tensor_scalar(
                dst, src, moments[:, i, 0:1], rstd[:, i:i + 1], ALU.subtract, ALU.mult), [r], "ln_done", cost=.4))
            return ln_done[-1]

        acc_loaded = {}

        def load_acc(half, tile, free=None, priority=None):
            acc_loaded[half, tile] = load(f"acc_in{tile}", acc[:, tile, :], x_tiles[half * HALF_TILES + tile], 256,
                                          [free], priority)

        stage_free = [None] * STAGE
        stage_count = {}
        part_ready = {}
        chunk_free = {}

        def take_stage(slots=ANY_SLOT):
            slot = slots[stage_count.get(slots, 0) % len(slots)]
            stage_count[slots] = stage_count.get(slots, 0) + 1
            free = stage_free[slot]
            assert free != "taken"
            stage_free[slot] = "taken"
            return slot, free

        def turn(b, src, rows, cols, waits, priority=None):
            def emit(e):
                for k in range(cols):
                    last = e.transpose(b.ap[:, k * rows:(k + 1) * rows], src[:, k * P:(k + 1) * P],
                                       ident[0:rows, 0:rows])
                return last
            return on_tensor(cols * T_MM / 2, emit, [*waits, table_in, b.free], "tile_turned",
                             priority=priority)

        def prepare_tile(kind, index, tt, b, early):
            slot, free = take_stage(ANY_SLOT if index < UNSHARED_CHUNKS else TOKEN_SLOTS)
            here = stage[:, slot, :]
            if kind == "x" and index < CHUNKS:
                tile = index * CHUNK_TILES + tt
                loaded = layer_norm(acc[:, tile, :], here, [acc_loaded[0, tile], free], now[0] - early)
            else:
                src = (x_tiles if kind == "x" else ctx_tiles)[index * CHUNK_TILES + tt]
                loaded = load(f"stage_in{slot}", here, src, 256, [free], now[0] - early - 3)
                if kind == "x":
                    loaded = layer_norm(here, here, [loaded], now[0] - early)
            filled = turn(b, here, P, KT, [loaded])
            stage_free[slot] = filled
            dst = (xT if kind == "x" else ctxT)[index % CHUNKS]
            src = b.ap[:, :].rearrange("p (k t) -> p k t", k=KT)
            high, low = (dst[:, part, :, tt * P:(tt + 1) * P] for part in (0, 1))
            h = put("scalar", now[0], lambda e: e.activation(high, src, ACT.Copy),
                    [filled, *chunk_free.get((kind, index % CHUNKS), [])], "tile_high")
            b.free = put("vector", now[0], lambda e: e.tensor_tensor(low, src, high.bitcast(F32), ALU.subtract), [h],
                         "tile_low")
            part_ready.setdefault((kind, index), []).append(b.free)

        raw_free = [None] * RAW
        raw_count = [0]

        def fetch(priority, src, k, high, low, free, engine=None):
            slot = raw_count[0] % RAW
            raw_count[0] += 1
            here = raw[:, slot, :] if k == 1 else raw[:, slot, :].rearrange("p (k n) -> p k n", k=k)
            loaded = load(f"raw_in{slot}", here, src, 256, [raw_free[slot]], priority - 4)
            h = put("scalar", priority, lambda e: e.activation(high, here, ACT.Copy), [loaded, free], "weight_high")
            engine = engine or ("vector" if k == 1 else "gpsimd")
            raw_free[slot] = put(engine, priority, lambda e: e.tensor_tensor(low, here, high.bitcast(F32), ALU.subtract),
                                 [h], f"weight_low_{engine}")
            return raw_free[slot]

        wq_ready, wk_ready, wv_ready, wo_ready = {}, {}, {}, {}

        def fetch_wq(priority, G, j, free=None, engine=None):
            col = ((G % KV_HEADS) * GROUP + j) * DH
            wq_ready[G, j] = fetch(priority, wq_rows[:, :, col:col + DH], KT, wq_s[j][:, 0], wq_s[j][:, 1], free, engine)

        def fetch_wk(priority, G, free=None):
            col = (G % KV_HEADS) * DH
            wk_ready[G] = fetch(priority, wk_rows[:, :, col:col + DH], KT, wk_s[:, 0], wk_s[:, 1], free)

        def fetch_wv(priority, G, free=None, engine=None):
            col = (G % KV_HEADS) * DH
            wv_ready[G] = [fetch(priority, wv_rows[:, k:k + 2, col:col + 2 * DH], 2, wv_s[:, 0, k:k + 2],
                                 wv_s[:, 1, k:k + 2], free, engine) for k in range(0, KT, 2)]

        def fetch_wo(priority, n, free=None):
            row = (n % HEADS) * DH
            w = wo_s[n % WO_SLOTS]
            wo_ready[n] = fetch(priority, wo[row:row + DH, :], 1, w[:, 0], w[:, 1], free)

        def unit(u):
            G, c = divmod(u, CHUNKS)
            return G, c, (G // KV_HEADS) * CHUNKS + c

        proj_count = [0]

        def project(width, stationary, moving, waits, b=None):
            if b is None:
                b = proj[proj_count[0] % 2]
                proj_count[0] += 1

            def emit(e):
                for k in range(KT):
                    for i, (s, m) in enumerate(SPLIT_PRODUCTS):
                        last = e.matmul(b.ap[:, 0:width], stationary(s, k), moving(m, k), start=(k == 0 and i == 0),
                                        stop=(k == KT - 1 and i == 2))
                return last
            return b, on_tensor(3 * KT * T_MM * width / 512, emit, [*waits, b.free], "projected")

        rope_added = []
        roped = {}
        scored = {}
        values_used = {}

        def rope(b, filled, dst, dst_free):
            i = len(rope_added)
            r = rot[:, i % 2, :]
            free = rope_added[i - 2] if i >= 2 else None
            half = DH // 2
            per_seq = [P, CHUNK_SEQS, SEQ]
            cos = tab[:, COS:COS + SEQ].unsqueeze(1).to_broadcast(per_seq)
            sin = tab[:, SIN:SIN + SEQ].unsqueeze(1).to_broadcast(per_seq)
            src, r3 = (v.rearrange("p (b s) -> p b s", s=SEQ) for v in (b.ap[:, :], r))

            def shift(e):
                e.activation(r[0:half, :], b.ap[half:DH, :], ACT.Copy)
                return e.activation(r[half:DH, :], b.ap[0:half, :], ACT.Copy)
            a = put("scalar", now[0], shift, [filled, free], "shifted_half", cost=1.0)
            s = put("gpsimd", now[0], lambda e: e.tensor_tensor(r3, r3, sin, ALU.mult), [a, table_in], "times_sin")
            c = put("vector", now[0], lambda e: e.tensor_tensor(dst, src, cos, ALU.mult), [a, dst_free, table_in],
                    "times_cos")
            b.free = c
            done = put("vector", now[0], lambda e: e.tensor_tensor(dst, dst, r3, ALU.add), [s, c], "rope_added")
            rope_added.append(done)
            return done

        def project_k(u):
            G, c, index = unit(u)
            b, filled = project(CHUNK, lambda s, k: wk_s[:, s, k, :], lambda m, k: ctxT[c][:, m, k, :],
                                [wk_ready[G], *part_ready["ctx", index]])
            roped[u, "k"] = rope(b, filled, k_r[:, u % 2, :].rearrange("p (b s) -> p b s", s=SEQ),
                                 scored.get(SUBS * (u - 2) + 1))
            chunk_free["ctx", c] = chunk_free.get(("ctx", c), [])[-CHUNK_TILES:] + [filled]
            if c == CHUNKS - 1 and G + 1 < GROUPS:
                fetch_wk(now[0] + 12, G + 1, filled)

        def project_q(u, j):
            G, c, index = unit(u)
            n = GROUP * u + j
            free = scored.get(SUBS * ((n - Q_SLOTS) // GROUP) + 1)
            b, filled = project(CHUNK, lambda s, k: wq_s[j][:, s, k, :], lambda m, k: xT[c][:, m, k, :],
                                [wq_ready[G, j], *part_ready["x", index]])
            roped[u, j] = rope(b, filled, q_r[:, n % Q_SLOTS // 2, :, n % 2, :], free)
            chunk_free["x", c] = chunk_free.get(("x", c), [])[-GROUP:] + [filled]
            if c == CHUNKS - 1 and G + 1 < GROUPS:
                fetch_wq(now[0] + 12, G + 1, j, filled)

        v_ready = {}

        def project_v(u, tt, b=None):
            G, c, index = unit(u)
            tile = c * CHUNK_TILES + tt
            b, filled = project(2 * DH, lambda s, k: ctxT[c][:, s, k, tt * P:(tt + 1) * P], lambda m, k: wv_s[:, m, k, :],
                                [*wv_ready[G], part_ready["ctx", index][tt]], b)
            chunk_free["ctx", c] = chunk_free.get(("ctx", c), [])[-CHUNK_TILES:] + [filled]
            h, low = None, None
            for twin, (own, other) in enumerate((TWIN_ROWS, TWIN_ROWS[::-1])):
                src, high = b.ap[own, 0:2 * DH], v_s[own, tile, twin, :]
                h = put("scalar", now[0], lambda e, high=high, src=src: e.activation(high, src, ACT.Copy),
                        [filled, values_used.get(SUBS * (u - 2) + 1)], "v_high", cost=.3, after=[h])
                low = put("vector", now[0], lambda e, high=high, src=src, dst=v_s[other, tile, twin, :]:
                          e.tensor_tensor(dst, src, high.bitcast(F32), ALU.subtract), [h], "v_low", cost=.35, after=[low])
            b.free = v_ready[G // 2, tile] = low
            if c == CHUNKS - 1 and tt == CHUNK_TILES - 1 and G + 2 < GROUPS:
                fetch_wv(now[0] + 35, G + 2, filled)

        normalised, probs_turned, probs_split, low_made = {}, {}, {}, {}
        out_used = {}
        x1_ready = {}

        def scores(k):
            u, s = divmod(k, SUBS)
            G, c, index = unit(u)

            def emit(e):
                for hp in range(HEAD_PAIRS):
                    for b in range(SUB_SEQS):
                        seq = s * SUB_SEQS + b
                        col = (hp * SUB_SEQS + b) * SEQ
                        two_heads = q_r[:, (GROUP * u + 2 * hp) % Q_SLOTS // 2, seq, :, :].rearrange("p h s -> p (h s)")
                        last = e.matmul(score.ap[:, col:col + SEQ], two_heads, k_r[:, u % 2, seq * SEQ:(seq + 1) * SEQ],
                                        start=True, stop=True)
                return last
            scored[k] = on_tensor(1.65, emit, [roped[u, w] for w in ("k", *range(GROUP))] + [score.free], "scored")
            i = k % 2
            p = prob[:, :]
            by_head = p.rearrange("p (h n) -> p h n", h=HEAD_PAIRS)
            by_row = p.rearrange("p (r k) -> p r k", r=ROWS)
            m = mask_sb[:, c, s * SUB_SEQS:(s + 1) * SUB_SEQS, :].rearrange("p b k -> p (b k)").unsqueeze(1).to_broadcast(
                [P, HEAD_PAIRS, SUB_SEQS * SEQ])
            masked = put("vector", now[0], lambda e: e.scalar_tensor_tensor(
                out=by_head, in0=score.ap[:, :].rearrange("p (h n) -> p h n", h=HEAD_PAIRS), scalar=SCALE, in1=m,
                op0=ALU.mult, op1=ALU.add), [scored[k], mask_in[index], probs_turned.get(k - 1)], "masked")
            score.free = masked
            if s == SUBS - 1 and G == KV_HEADS - 1:
                load_mask(index + CHUNKS, now[0] + 5, masked)
            a = put("vector", now[0], lambda e: e.tensor_reduce(neg_max[:, i, :], by_row, AX.X, ALU.max, negate=True),
                    [masked], "neg_max")
            b = put("gpsimd", now[0], lambda e: e.tensor_tensor(
                by_row, by_row, neg_max[:, i, :].unsqueeze(2).to_broadcast([P, ROWS, SEQ]), ALU.add), [a], "less_max")
            ex = put("scalar", now[0], lambda e: e.activation(p, p, ACT.Exp), [b], "exponentials")
            sm = put("vector", now[0], lambda e: e.tensor_reduce(row_sum[:, i, :], by_row, AX.X, ALU.add), [ex], "row_sum")
            inv = put("vector", now[0], lambda e: e.reciprocal(row_inv[:, i, :], row_sum[:, i, :]), [sm], "row_inv",
                      cost=T_SMALL)
            normalised[k] = put("gpsimd", now[0], lambda e: e.tensor_tensor(
                by_row, by_row, row_inv[:, i, :].unsqueeze(2).to_broadcast([P, ROWS, SEQ]), ALU.mult), [inv], "normalised")

        def turn_probs(k):
            def emit(e):
                for bp in range(PAIRS):
                    for hp in range(HEAD_PAIRS):
                        src = (hp * PAIRS + bp) * P
                        dst = (bp * HEAD_PAIRS + hp) * P
                        last = e.transpose(turned.ap[:, dst:dst + P], prob[:, src:src + P], ident)
                return last
            probs_turned[k] = on_tensor(.43, emit, [normalised[k], turned.free], "probs_turned")
            h, low = None, None
            for twin, rows in enumerate(TWIN_ROWS):
                src = turned.ap[rows, :]

                def twice(e, src=src, twin=twin):
                    e.activation(p_high[TWIN_ROWS[1 - twin], twin, :], src, ACT.Copy)
                    return e.activation(p_high[TWIN_ROWS[twin], twin, :], src, ACT.Copy)
                h = put("scalar", now[0], twice, [probs_turned[k], values_used.get(k - 1)], "probs_high", cost=1.0,
                        after=[h])
                low = put("vector", now[0], lambda e, rows=rows, src=src, twin=twin: e.tensor_tensor(
                    p_low[rows, :], src, p_high[rows, twin, :].bitcast(F32), ALU.subtract),
                    [h, values_used.get(k - 1)], "probs_low", after=[low])
            turned.free = probs_split[k] = low

        def times_values(k):
            u, s = divmod(k, SUBS)
            G, c, index = unit(u)
            tiles = [c * CHUNK_TILES + s * PAIRS + bp for bp in range(PAIRS)]
            head = slice((G % 2) * DH, (G % 2 + 1) * DH)

            def highs(e):
                for bp in range(PAIRS):
                    cols = slice(bp * GROUP * SEQ, (bp + 1) * GROUP * SEQ)
                    for twin in range(2):
                        last = e.matmul(attn[twin].ap[:, cols], v_s[:, tiles[bp], twin, head], p_high[:, twin, cols],
                                        start=(bp == 0), stop=False, skip_group_check=True)
                return last

            def lows(e):
                for bp in range(PAIRS):
                    cols = slice(bp * GROUP * SEQ, (bp + 1) * GROUP * SEQ)
                    for twin, rows in enumerate(TWIN_ROWS):
                        last = e.matmul(attn[twin].ap[:, cols], v_s[rows, tiles[bp], twin, head], p_low[rows, cols],
                                        start=False, stop=True, skip_group_check=True)
                return last
            first = on_tensor(2 * T_MM, highs, [probs_split[k], attn[0].free, attn[1].free] +
                              [v_ready[G // 2, t] for t in tiles], "values_times_high")
            values_used[k] = on_tensor(2 * T_MM, lows, [], "values_used", after=[first])
            for twin in range(2):
                src = attn[twin].ap[:, :].rearrange("p (b h q) -> p b h q", b=PAIRS, h=GROUP)
                high, low = (o_s[:, part, :, :, SEQ * twin:SEQ * twin + SEQ] for part in (0, 1))
                h = put("scalar", now[0], lambda e, high=high, src=src: e.activation(high, src, ACT.Copy),
                        [values_used[k], out_used.get(k - 1)], "out_high")
                attn[twin].free = low_made[k, twin] = put(
                    "vector", now[0], lambda e, high=high, low=low, src=src:
                    e.tensor_tensor(low, src, high.bitcast(F32), ALU.subtract), [h], "out_low")

        def project_out(k, bp):
            u, sub = divmod(k, SUBS)
            G, c, index = unit(u)
            last_use = c == CHUNKS - 1 and sub == SUBS - 1 and bp == PAIRS - 1
            used = None
            b = attn[0] if k == UNITS * SUBS - 1 and bp == PAIRS - 1 else y
            for h in range(GROUP):
                n = G * GROUP + h
                w = wo_s[n % WO_SLOTS]

                def emit(e, h=h, w=w):
                    for i, (s, m) in enumerate(SPLIT_PRODUCTS):
                        last = e.matmul(b.ap[:, :], o_s[:, s, bp, h, :], w[:, m, :], start=(h == 0 and i == 0),
                                        stop=(h == GROUP - 1 and i == 2))
                    return last
                used = on_tensor(3 * T_MM, emit, [wo_ready[n], low_made[k, 0], low_made[k, 1], b.free], "out_projected",
                                 after=[used])
                if last_use and n + WO_SLOTS < GROUPS * GROUP:
                    fetch_wo(now[0], n + WO_SLOTS, used)
            out_used[k] = used
            tile = c * CHUNK_TILES + sub * PAIRS + bp
            half = G // KV_HEADS
            here = acc[:, tile, :]
            b.free = x1_ready[half, tile] = put("vector", now[0], lambda e: e.scalar_tensor_tensor(
                out=here, in0=b.ap[:, :], scalar=gates_t[:, 0:1], in1=here, op0=ALU.mult, op1=ALU.add),
                [used, gates_ready, acc_loaded[half, tile], x1_ready.get((half, tile))], "x1_added")

        stores = []

        def experts(half, tile, b, priority):
            here = acc[:, tile, :]
            slot, free = take_stage(EXPERT_SLOTS if half + 1 < HALVES else ANY_SLOT)
            at = stage[:, slot, :]
            normed = layer_norm(here, at, [x1_ready[half, tile], free], priority)
            t = turn(b, at, P, KT, [normed], priority)
            b.free = copied = put("scalar", priority, lambda e: e.activation(at, b.ap[:, :], ACT.Copy), [t], "x1_turned")

            def route(e):
                for k in range(KT):
                    last = e.matmul(b.ap[:, 0:ROUTED], at[:, k * P:(k + 1) * P], routedT[:, k, :], start=(k == 0),
                                    stop=(k == KT - 1))
                return last
            routed = on_tensor(KT * 4 * ROUTED / 2400, route, [copied, experts_ready, b.free], "routed", priority=priority)
            best, rank, ranks, weight = (top[:, slot, a:b] for a, b in
                                         ((0, 1), (1, 2), (2, 2 + EXPERTS), (2 + EXPERTS, 2 + 2 * EXPERTS)))
            logits = b.ap[:, 0:EXPERTS]
            small_step = {"cost": T_SMALL}
            m = put("vector", priority, lambda e: e.tensor_reduce(best, logits, AX.X, ALU.max), [routed], "top_logit",
                    **small_step)
            r = put("vector", priority, lambda e: e.scalar_tensor_tensor(
                out=ranks, in0=logits, scalar=best, in1=tab[:, RANKS:RANKS + EXPERTS], op0=ALU.is_equal, op1=ALU.mult),
                [m, table_in], "top_ranks", **small_step)
            f = put("vector", priority, lambda e: e.tensor_reduce(rank, ranks, AX.X, ALU.max), [r], "top_rank", **small_step)
            w = put("vector", priority, lambda e: e.tensor_scalar(weight, ranks, rank, best, ALU.is_equal, ALU.mult), [f],
                    "top_weight", **small_step)
            wh, whT = at[:, 0:ER], at[:, ER:ER + P]
            by_expert = "p (e r) -> p e r"
            b.free = weighted = put("vector", priority, lambda e: e.tensor_tensor(
                wh.rearrange(by_expert, e=EXPERTS), b.ap[:, EXPERTS:ROUTED].rearrange(by_expert, e=EXPERTS),
                weight.unsqueeze(2).to_broadcast([P, EXPERTS, RANK]), ALU.mult), [w], "weighted", cost=.25)
            t = turn(b, wh, P, 1, [weighted], priority)
            b.free = copied = put("scalar", priority, lambda e: e.activation(whT, b.ap[:, 0:P], ACT.Copy), [t],
                                  "weighted_turned", cost=.25)
            stage_free[slot] = mixed = on_tensor(4 * T_MM, lambda e: e.matmul(
                b.ap[:, :], whT, lora_bT[:, :], start=True, stop=True), [copied, experts_ready, b.free], "mixed", priority=priority)
            b.free = done = put("vector", priority, lambda e: e.scalar_tensor_tensor(
                out=here, in0=b.ap[:, :], scalar=gates_t[:, 1:2], in1=here, op0=ALU.mult, op1=ALU.add),
                [mixed, gates_ready], "out_ready")
            stored = load(f"stored{tile}", out_tiles[half * HALF_TILES + tile], here, 256, [done])
            stores.append(stored)
            if half + 1 < HALVES:
                load_acc(half + 1, tile, stored)

        def expert_weights():
            (sa, free_a), (sr, free_r), (sbw, free_b) = take_stage(), take_stage(), take_stage()
            a_nat, r_nat, b_nat = stage[:, sa, :], stage[0:EXPERTS, sr, :], stage[:, sbw, :]
            a_in = load("lora_a_in", a_nat, lora_a.rearrange("e r d -> (e r) d"), 256, [free_a])
            r_in = load("route_w_in", r_nat, route_w, 16, [free_r])
            b4 = b_nat.rearrange("p (t e r) -> p t e r", t=KT, e=EXPERTS)
            b_in = None
            for tt in range(KT):
                b_in = load("lora_b_in", b4[:, tt], lora_b[:, tt * P:(tt + 1) * P, :].rearrange("e o r -> o e r"), 128,
                            [free_b], after=[b_in])

            def place(src, rows, dst, arrived):
                t = turn(small, src, rows, KT, [arrived])
                small.free = put("vector", now[0], lambda e: e.tensor_copy(
                    dst, small.ap[:, 0:KT * rows].rearrange("p (k r) -> p k r", k=KT)), [t], "expert_weights")
                return t
            stage_free[sa] = place(a_nat, P, routedT[:, :, EXPERTS:ROUTED], a_in)
            stage_free[sr] = place(r_nat, EXPERTS, routedT[:, :, 0:EXPERTS], r_in)
            stage_free[sbw] = place(b_nat, P, lora_bT[:, :].rearrange("p (k r) -> p k r", k=KT), b_in)
            return small.free

        prologue_banks = [small, score, turned, y]

        def prepare_chunk(index, kinds, banks, early):
            for i, (kind, tt) in enumerate((kind, tt) for kind in kinds for tt in range(CHUNK_TILES)):
                prepare_tile(kind, index, tt, banks[i % len(banks)], early)

        for tile in range(HALF_TILES):
            load_acc(0, tile, priority=-4 if tile < CHUNK_TILES else 8)
        fetch_wv(-8, 0, engine="vector")
        fetch_wk(-6, 0)
        prepare_chunk(0, ["ctx", "x"], prologue_banks, 10)
        for j in range(GROUP):
            fetch_wq(1 + j, 0, j, engine="vector" if j < 2 else "gpsimd")
        for tt in range(CHUNK_TILES):
            project_v(0, tt, attn[tt % 2])
        project_k(0)
        load_mask(0, 10)
        load_mask(1, 30)
        for j in range(GROUP):
            project_q(0, j)
            if j == 0:
                prepare_chunk(1, ["ctx", "x"], [small, turned], 12)
        for n in range(WO_SLOTS):
            fetch_wo(now[0] + n, n)
        expert_banks = [[small] * HALF_TILES, [small, small, small, proj[0], proj[1], score, proj[0], turned]]

        for k in range(UNITS * SUBS + 1):
            u, s = divmod(k, SUBS)
            jobs = []
            nxt = u + 1
            if nxt < UNITS:
                if s == 0:
                    jobs = [lambda: project_k(nxt), lambda: project_q(nxt, 0), lambda: project_q(nxt, 1)]
                else:
                    jobs = [lambda: project_q(nxt, 2), lambda: project_q(nxt, 3)]
                if unit(nxt)[0] % 2 == 0:
                    jobs += [lambda: project_v(nxt, 2 * s), lambda: project_v(nxt, 2 * s + 1)]

            def job():
                if jobs:
                    jobs.pop(0)()

            if k < UNITS * SUBS:
                scores(k)
            job()
            if k >= 1:
                project_out(k - 1, 0)
            job()
            if k < UNITS * SUBS:
                turn_probs(k)
            if k >= 1:
                project_out(k - 1, 1)
            while jobs:
                job()
            if k < UNITS * SUBS:
                times_values(k)
            if k == 1:
                experts_ready = expert_weights()
            if u in (KV_HEADS * CHUNKS - 2, KV_HEADS * CHUNKS - 1):
                index = u - (KV_HEADS - 1) * CHUNKS + CHUNKS
                prepare_chunk(index, ["ctx" if s == 0 else "x"],
                              [small, turned] if index < UNSHARED_CHUNKS else [turned], 6)
            for half in range(HALVES):
                for c in range(CHUNKS):
                    done = ((half * KV_HEADS + KV_HEADS - 1) * CHUNKS + c) * SUBS
                    if k - 1 - done in (0, 1):
                        for bp in range(PAIRS):
                            n = k - 1 - done
                            tile = c * CHUNK_TILES + n * PAIRS + bp
                            experts(half, tile, expert_banks[half][tile], now[0] + EXPERT_DELAY[half][tile // PAIRS])

        last_stores = put("sync", now[0] + 1e6, lambda e: e.nop(), stores, "all_stored")
        plan.arrange()
        block = stack.enter_context(nc.Block())

        @block.sync
        def _(eng):
            plan.emit("sync", eng)

        @block.tensor
        def _(eng):
            plan.emit("tensor", eng)

        @block.vector
        def _(eng):
            plan.emit("vector", eng)

        @block.scalar
        def _(eng):
            plan.emit("scalar", eng)

        @block.gpsimd
        def _(eng):
            plan.emit("gpsimd", eng)


def constants():
    half = DH // 2
    inv_freq = np.float32(1.0) / np.float32(ROPE_BASE) ** (np.arange(0, DH, 2, dtype=np.float32) / np.float32(DH))
    angle = np.arange(SEQ, dtype=np.float32)[None, :] * inv_freq.astype(np.float32)[:, None]
    table = np.zeros((P, TABLE), np.float32)
    table[:, COS:COS + SEQ] = np.concatenate([np.cos(angle), np.cos(angle)])
    table[:, SIN:SIN + SEQ] = np.concatenate([-np.sin(angle), np.sin(angle)])
    table[:, IDENT:IDENT + P] = np.eye(P, dtype=np.float32)
    table[:, RANKS:] = np.arange(EXPERTS, 0, -1, dtype=np.float32)
    return table


_INS = ['x', 'ctx_4096', 'mask_BxSxS2_ff0', 'g_xattn', 'g_ffn', 'L0_xattn_wq', 'L0_xattn_wk', 'L0_xattn_wv',
        'L0_xattn_wo', 'L0_ffn_route_w', 'L0_ffn_A', 'L0_ffn_Bw']


def kernel(**inputs):
    import concourse.bacc as bacc
    from concourse.bass_utils import run_bass_kernel_spmd

    nc = bacc.Bacc("TRN2", target_bir_lowering=False, num_devices=1)
    arrays, args = {}, []
    for name in _INS:
        a = np.ascontiguousarray(inputs[name])
        arrays[f"in_{name}"] = a
        args.append(nc.dram_tensor(f"in_{name}", a.shape, mybir.dt.from_np(a.dtype), kind="ExternalInput").ap())
    table = constants()
    arrays["table"] = table
    args.append(nc.dram_tensor("table", table.shape, F32, kind="ExternalInput").ap())
    args.append(nc.dram_tensor("out", (BATCH, SEQ, DM), F32, kind="ExternalOutput").ap())
    build(nc, *args)
    r = run_bass_kernel_spmd(nc, [arrays], core_ids=[0])
    return r.results[0]["out"]
```
